# Optimizing a Trainium2 kernel written in Bass

```python
import numpy as np
import jax
import jax.numpy as jnp

def _softmax(x, axis=-1):
    return jax.nn.softmax(x, axis=axis)

def _gelu(x):
    return jax.nn.gelu(x, approximate=True)

def _silu(x):
    return jax.nn.silu(x)

def _sigmoid(x):
    return jax.nn.sigmoid(x)

def _layernorm(x, axis=-1, eps=1e-05):
    m = jnp.mean(x, axis=axis, keepdims=True)
    v = jnp.var(x, axis=axis, keepdims=True)
    return (x - m) / jnp.sqrt(v + eps)

def _scatter_add(tgt, idx, src, axis=0):
    return tgt.at[idx].add(src)

def _segment_sum(src, seg, n):
    return jax.ops.segment_sum(src, seg, n)
kernel_name = 'mk_adj_preln_d2_adj_r2_a1f990'

def setup_inputs(seed: int=0):
    np.random.seed(seed)
    _w = jnp.asarray

    def _rec_inputs():
        import jax
        import jax.numpy as jnp
        _gk = jax.random.key(seed)
        x = -0.0005207 + 1.001 * jax.random.normal(jax.random.fold_in(_gk, 1), (4096, 128), jnp.float32)
        _a = jax.random.bernoulli(jax.random.fold_in(_gk, 2), 0.00195312, (4096, 4096))
        _a = jnp.logical_or(_a, jnp.eye(4096, dtype=bool))
        _af = _a.astype(jnp.float32)
        adj = _af
        return (x, adj)
    x, adj = _rec_inputs()

    def _L0_gnn_setup():
        import jax, jax.numpy as jnp
        import numpy as np
        N = 4096
        D_IN = 128
        D_OUT = 128
        key = jax.random.key(seed)
        k_x, k_a, k_w, k_bias = jax.random.split(key, 4)
        x = jax.random.normal(k_x, (N, D_IN), dtype=jnp.float32)
        A_shape = jax.random.randint(k_a, (N, N), 0, 2).astype(jnp.float32)
        A_shape = A_shape.at[jnp.arange(N), jnp.arange(N)].set(1.0)
        lim = 1.0 / np.sqrt(D_IN)
        W = jax.random.uniform(k_w, (D_OUT, D_IN), jnp.float32, -lim, lim)
        bias = jax.random.uniform(k_bias, (D_OUT,), jnp.float32, -lim, lim)
        b = jnp.ones((1,), dtype=jnp.float32)
        return {'x': x, 'A_shape': A_shape, 'W': W, 'bias': bias, 'b': b}
    _L0_gnn_all = _L0_gnn_setup()
    _L0_gnn_in = {k: v for k, v in _L0_gnn_all.items() if k in ('W', 'bias', 'b')}
    del _L0_gnn_all

    def _L1_gnn_setup():
        import jax, jax.numpy as jnp
        import numpy as np
        EPS = 1e-08
        NEG = -10000000000.0

        def _l2norm(v):
            n = jnp.sqrt(jnp.sum(v * v, axis=-1, keepdims=True))
            return v / jnp.maximum(n, EPS)
        key = jax.random.key(seed)
        k1, k2, k3 = jax.random.split(key, 3)
        N, M, D = (4096, 4096, 128)
        x = jax.random.normal(k1, (N, D), dtype=jnp.float32)
        y = jax.random.normal(k2, (M, D), dtype=jnp.float32)
        adj = (jax.random.uniform(k3, (N, M)) < 0.02).astype(jnp.float32)
        adj = adj.at[jnp.arange(N), jnp.arange(N) % M].set(1.0)
        return {'x': x, 'y': y, 'adj': adj}
    _L1_gnn_all = _L1_gnn_setup()
    _L1_gnn_in = {k: v for k, v in _L1_gnn_all.items() if k in ('y',)}
    del _L1_gnn_all
    return {'x': x, 'adj': adj, 'L0_gnn_W': _L0_gnn_in['W'], 'L0_gnn_bias': _L0_gnn_in['bias'], 'L0_gnn_b': _L0_gnn_in['b'], 'L1_gnn_y': _L1_gnn_in['y']}

def reference(x, adj, L0_gnn_W, L0_gnn_bias, L0_gnn_b, L1_gnn_y):
    import jax
    import jax.numpy as jnp

    def _L0_gnn_ref(x, A_shape, W, bias, b):
        import jax, jax.numpy as jnp
        import numpy as np
        N = 4096
        D_IN = 128
        D_OUT = 128
        y = jnp.linalg.norm(x, axis=-1, keepdims=True)
        A = x @ x.T / (y @ y.T)
        A = A * b
        A = jnp.tanh(A / 8.0) * 8.0
        A = jnp.exp(A) * A_shape
        A = A / jnp.sum(A, axis=-1, keepdims=True)
        x = A @ x
        return x @ W.T + bias

    def _L1_gnn_ref(x, y, adj):
        import jax, jax.numpy as jnp
        import numpy as np
        EPS = 1e-08
        NEG = -10000000000.0

        def _l2norm(v):
            n = jnp.sqrt(jnp.sum(v * v, axis=-1, keepdims=True))
            return v / jnp.maximum(n, EPS)
        cos = _l2norm(x) @ _l2norm(y).T
        masked = cos + (1.0 - adj) * NEG
        P = jax.nn.softmax(masked, axis=-1)
        return 0.5 * (P @ y) + 0.5 * x
    h = jnp.maximum(_layernorm(x, axis=-1), 0.0)
    x = x + _L0_gnn_ref(h, adj, L0_gnn_W, L0_gnn_bias, L0_gnn_b)
    h = jnp.maximum(_layernorm(x, axis=-1), 0.0)
    x = x + _L1_gnn_ref(h, L1_gnn_y, adj)
    return x

_drawn_inputs = setup_inputs


def setup_inputs(seed=0):
    import zlib

    import numpy as np

    out = dict(_drawn_inputs(seed))
    spreads = {}
    factors = {}
    for name, (base, spread) in spreads.items():
        noise = np.random.default_rng([zlib.crc32(name.encode()), seed]).standard_normal(out[name].shape)
        drawn = base * np.exp(spread * noise) if base else spread * noise
        out[name] = jnp.asarray(drawn.astype(out[name].dtype))
    for name, factor in factors.items():
        out[name] = (out[name] * factor).astype(out[name].dtype)
    return out
```

```python
from contextlib import ExitStack

import concourse.bass as bass
from concourse import mybir

F32 = mybir.dt.float32
F16 = mybir.dt.float16
BF16 = mybir.dt.bfloat16
ALU = mybir.AluOpType
ACT = mybir.ActivationFunctionType

P = 128
LN_EPS = 1e-5
NORM_EPS = 1e-8
UNIT = 64.0
VALUE = 16.0
COS = 1.0 / (UNIT * UNIT)
LOG_SHIFT = 11 * 0.6931471805599453


def two_layers(nc, x, adj, W, bias, b, y, out):
    N, D = x.shape
    NT = N // P
    SUB = 4
    BLK = SUB * P
    NB = N // BLK
    PAIRS = NT // 2
    UNROLL = 4
    ITERS = PAIRS // UNROLL
    CHUNK = 4 * P
    VCOL = 2 * D + 2
    LAG = 2
    assert D == P and PAIRS % UNROLL == 0

    with ExitStack() as ctx:
        def sb(name, shape, dt):
            return ctx.enter_context(nc.sbuf_tensor(name, shape, dt))

        def ps(name, shape, dt):
            return ctx.enter_context(nc.psum_tensor(name, shape, dt))

        def sem(name):
            return ctx.enter_context(nc.semaphore(name))

        keys_hi = [sb(f"keys_hi{l}", [P, N], F16) for l in range(2)]
        keys_lo = [sb(f"keys_lo{l}", [P, N], F16) for l in range(2)]
        vals = [sb(f"vals{l}", [P, NT, VCOL], F16) for l in range(2)]
        mask = sb("mask", [P, 2, NT, BLK], BF16)
        adj_in = [sb(f"adj_in{i}", [P, SUB, CHUNK], F32) for i in range(2)]
        expo = [sb(f"expo{i}", [P, 2 * BLK], F32) for i in range(2)]
        wts = [sb(f"wts{i}", [P, 2 * BLK], F32) for i in range(UNROLL)]
        wts_lo = [sb(f"wts_lo{i}", [P, 2 * BLK], F16) for i in range(UNROLL)]
        q_next = sb("q_next", [P, 2, BLK], F16)
        q_now = sb("q_now", [P, 2, BLK], F16)
        half_h = sb("half_h", [P, SUB, D], F32)
        base = sb("base", [P, SUB, D], F32)
        raw = [sb(f"raw{l}", [P, SUB, D + 1], F32) for l in range(2)]
        x_res = sb("x_res", [P, SUB, D], F32)
        x1 = sb("x1", [P, SUB, D], F32)
        h1 = sb("h1", [P, SUB, D], F32)
        hn1 = sb("hn1", [P, SUB, D], F32)
        sq = sb("sq", [P, SUB, D], F32)
        res = sb("res", [P, SUB, D], F32)
        stats = sb("stats", [P, SUB, 6], F32)
        mv = sb("mv", [P, SUB, 2], F32)
        rstd = sb("rstd", [P, SUB], F32)
        ss = sb("ss", [P, SUB], F32)
        inv = sb("inv", [P, SUB], F32)
        inv_sum = [sb(f"inv_sum{l}", [P, SUB], F32) for l in range(2)]
        xg = [wts[g][:, 0:BLK].rearrange("p (u d) -> p u d", u=SUB) for g in range(2)]
        yg = [wts[g][:, BLK:2 * BLK].rearrange("p (u d) -> p u d", u=SUB) for g in range(2)]
        hg = [wts[2 + g][:, 0:BLK].rearrange("p (u d) -> p u d", u=SUB) for g in range(2)]
        yng = [wts[2 + g][:, BLK:2 * BLK].rearrange("p (u d) -> p u d", u=SUB) for g in range(2)]
        hT = [expo[g][:, 0:BLK] for g in range(2)]
        vg = [expo[g][:, BLK:2 * BLK].rearrange("p (u d) -> p u d", u=SUB) for g in range(2)]
        stats_g = [sb(f"stats_g{g}", [P, SUB, 6], F32) for g in range(2)]
        mv_g = [sb(f"mv_g{g}", [P, SUB, 2], F32) for g in range(2)]
        col_g = [sb(f"col_g{g}", [P, 6, SUB], F32) for g in range(2)]
        w_in = sb("w_in", [P, D], F32)
        w_T = sb("w_T", [P, D], F32)
        bias_row = sb("bias_row", [P, D], F32)
        b_col = sb("b_col", [P, 1], F32)
        tanh_scale = sb("tanh_scale", [P, 1], F32)
        shift_col = sb("shift_col", [P, 1], F32)
        ident = sb("ident", [P, P], F32)
        ident_b = sb("ident_b", [P, P], BF16)
        neg_half = sb("neg_half", [P, SUB], F32)
        pos_half = sb("pos_half", [P, SUB], F32)
        eps_col = sb("eps_col", [P, SUB], F32)
        value_col = sb("value_col", [P, 1], F32)

        S = [ps(f"S{i}", [P, 2 * BLK], F32) for i in range(2)]
        O = ps("O", [P, 2, 512], F32)
        AT = ps("AT", [P, 2 * BLK], BF16)
        TQ = ps("TQ", [P, BLK], F32)

        names = """const_loaded zeros_ready idents_ready scale_ready wT_ready w_ready
            x_loaded0 x_loaded1 y_loaded0 y_loaded1 g_stats g_mv g_var g_rstd g_pre g_h g_ss g_inv g_norm g_ssy_sum g_ssy g_invy
            g_unit g_T g_hi g_lo g_hT g_v g_vs g_vhi_x g_vhi_y g_vlo
            adj_loaded0 adj_loaded1 at_ready mask_ready scores_ready scores_free exp_ready
            wts_ready lo_ready pv_done o_half o_free
            xres_loaded xres_ready inv_sum_ready x1_ready stats_ready mv_ready var_ready rstd_ready hpre_ready
            h_ready ss_sum_ready ss_ready inv_ready hn_ready half_ready base_ready q_T q_hi q_ready moved
            inv_out_ready inv_half_ready res_ready stored""".split()
        s_ = {n: sem(n) for n in names}

        def wait(eng, name, value):
            if isinstance(value, int) and value <= 0:
                return
            eng.wait_ge(s_[name], value)

        adj_blocks = adj.rearrange("(s u p) j -> s p u j", u=SUB, p=P)
        x_blocks = x.rearrange("(s u p) d -> s p u d", u=SUB, p=P)
        y_blocks = y.rearrange("(s u p) d -> s p u d", u=SUB, p=P)
        out_blocks = out.rearrange("(s u p) d -> s p u d", u=SUB, p=P)

        def block_of(dram, s):
            return dram[bass.ds(s, 1)].rearrange("s p u d -> (s p) u d") if not isinstance(s, int) else dram[s]

        def phases(eng, run):
            run(0, 0, 0, None)
            run(0, 1, 1, 0)
            run(1, 0, 2, 0)
            with eng.Fori(2, NB) as s:
                run(0, s, 2 * s - 1, 1)
                run(1, s - 1, 2 * s, 0)
            run(1, NB - 1, 2 * NB - 1, 1)

        def pairs(eng, step):
            for kk in range(UNROLL):
                step(0, kk, True)
            with eng.Fori(1, ITERS) as it:
                for kk in range(UNROLL):
                    step(it, kk, False)

        def mask_pair(s, k):
            first = (s % 2) * NT + 2 * k
            return mask[:, :, :, :].rearrange("p a t i -> p (a t) i")[:, bass.ds(first, 2), :]

        def block_before(layer, s, before):
            return {(0, 0): s - 1, (1, 0): s + 1, (0, 1): s - 2, (1, 1): s - 1}[(layer, before)]

        block = ctx.enter_context(nc.Block())

        @block.sync
        def _(sp):
            sp.dma_start(w_in[:, :], W).then_inc(s_["const_loaded"], 16)
            sp.dma_start(bias_row[:, :], bias.rearrange("(a d) -> a d", a=1).to_broadcast((P, D))).then_inc(
                s_["const_loaded"], 16)
            sp.dma_start(b_col[:, :], b.rearrange("(a d) -> a d", a=1).to_broadcast((P, 1))).then_inc(
                s_["const_loaded"], 16)

            def load_group(g, i):
                if not isinstance(g, int):
                    sp.wait_ge(s_["g_vlo"], 2 * (g - 1))
                sp.dma_start(xg[i], block_of(x_blocks, g)).then_inc(s_[f"x_loaded{i}"], 16)
                sp.dma_start(yg[i], block_of(y_blocks, g)).then_inc(s_[f"y_loaded{i}"], 16)

            def load_chunk(s, c):
                n = (NT // 4) * s + c
                if not (isinstance(n, int) and n < 2):
                    sp.wait_ge(s_["at_ready"], 2 * n - 2)
                sp.dma_start(adj_in[c % 2][:, :, :],
                             block_of(adj_blocks, s)[:, :, c * CHUNK:(c + 1) * CHUNK]).then_inc(
                    s_[f"adj_loaded{c % 2}"], 16)

            def load_rows(s):
                for c in range(NT // 4):
                    load_chunk(s, c)
                sp.wait_ge(s_["x1_ready"], s)
                sp.dma_start(x_res[:, :, :], block_of(x_blocks, s)).then_inc(s_["xres_loaded"], 16)

            def store(s):
                sp.wait_ge(s_["res_ready"], s + 1)
                sp.dma_start(block_of(out_blocks, s), res[:, :, :]).then_inc(s_["stored"], 16)

            load_group(0, 0)
            load_group(1, 1)
            load_chunk(0, 0)
            load_chunk(0, 1)
            with sp.Fori(1, NB // 2) as g:
                load_group(2 * g, 0)
                load_group(2 * g + 1, 1)
            for c in range(2, NT // 4):
                load_chunk(0, c)
            sp.dma_start(x_res[:, :, :], x_blocks[0]).then_inc(s_["xres_loaded"], 16)
            load_rows(1)
            load_rows(2)
            with sp.Fori(3, NB) as s:
                store(s - 3)
                load_rows(s)
            for s in range(NB - 3, NB):
                store(s)
            sp.wait_ge(s_["stored"], 16 * NB)

        @block.tensor
        def _(pe):
            pe.wait_ge(s_["idents_ready"], 1)
            pe.wait_ge(s_["const_loaded"], 48)
            nc.tensor.transpose(TQ[:, 0:P], w_in[:, :], ident[:, :]).then_inc(s_["wT_ready"], 1)

            with pe.Fori(0, NB // 2) as g2:
                for i in range(2):
                    g = 2 * g2 + i
                    pe.wait_ge(s_["g_unit"], 1 + g)
                    for u in range(SUB):
                        nc.tensor.transpose(S[i][:, u * P:(u + 1) * P], hg[i][:, u, :], ident[:, :])
                    for u in range(SUB):
                        last = nc.tensor.transpose(S[i][:, BLK + u * P:BLK + (u + 1) * P], yng[i][:, u, :],
                                                   ident[:, :])
                    last.then_inc(s_["g_T"], 1)
                for i in range(2):
                    g = 2 * g2 + i
                    pe.wait_ge(s_["g_hT"], 1 + g)
                    if i == 0:
                        pe.wait_ge(s_["w_ready"], 1)
                    for u in range(SUB):
                        last = nc.tensor.matmul(O[:, i, u * P:(u + 1) * P], hT[i][:, u * P:(u + 1) * P],
                                                w_T[:, :], start=True, stop=True)
                    last.then_inc(s_["g_v"], 1)

            def scores(layer, s, G, k, kk):
                wait(pe, "scores_free", G - 1)
                dst = S[kk % 2]
                for jj in range(2):
                    cols = bass.ds((2 * k + jj) * P, P)
                    k_hi, k_lo = keys_hi[layer][:, cols], keys_lo[layer][:, cols]
                    if layer == 0:
                        q_hi = keys_hi[0][:, bass.ds(s * BLK, BLK)]
                        q_lo = keys_lo[0][:, bass.ds(s * BLK, BLK)]
                    else:
                        q = q_next if isinstance(s, int) and s == NB - 1 else q_now
                        q_hi, q_lo = q[:, 0, :], q[:, 1, :]
                    o = dst[:, jj * BLK:(jj + 1) * BLK]
                    nc.tensor.matmul(o, k_hi, q_hi, start=True, stop=False)
                    nc.tensor.matmul(o, k_hi, q_lo, start=False, stop=False)
                    last = nc.tensor.matmul(o, k_lo, q_hi, start=False, stop=True)
                last.then_inc(s_["scores_ready"], 1)

            def turn_adj(s, it, kk):
                if kk % 2 == 0:
                    pe.wait_ge(s_[f"adj_loaded{kk // 2}"], 16 * (ITERS * s + it + 1))
                wait(pe, "mask_ready", PAIRS * s + UNROLL * it + kk)
                src = adj_in[(kk // 2) % 2][:, :, :].bitcast(BF16).rearrange("p u (j two) -> p u two j", two=2)
                for jj in range(2):
                    for u in range(SUB):
                        c0 = (2 * (kk % 2) + jj) * P
                        last = nc.tensor.transpose(AT[:, (jj * SUB + u) * P:(jj * SUB + u + 1) * P],
                                                   src[:, u, 1, c0:c0 + P], ident_b[:, :])
                last.then_inc(s_["at_ready"], 1)

            def products(layer, p, G, k, slot):
                first = isinstance(k, int) and k == 0
                final = isinstance(k, int) and k == PAIRS - 1
                if first:
                    wait(pe, "o_free", 2 * p)
                pe.wait_ge(s_["lo_ready"], G + 1)
                hi = wts[slot][:, :].bitcast(BF16).rearrange("p (c two) -> p two c", two=2)
                for u in range(SUB):
                    o = O[:, u // 2, (u % 2) * (D + 1):(u % 2 + 1) * (D + 1)]
                    for jj in range(2):
                        c0 = jj * BLK + u * P
                        tile = 2 * k + jj
                        if isinstance(k, int):
                            v = vals[layer][:, tile, :]
                        else:
                            v = vals[layer][:, bass.ds(tile, 1), :].rearrange("p a c -> p (a c)")
                        w_hi, w_lo = hi[:, 1, c0:c0 + P], wts_lo[slot][:, c0:c0 + P]
                        nc.tensor.matmul(o, w_hi, v[:, 0:D + 1], start=first and jj == 0 and u % 2 == 0,
                                         stop=False, skip_group_check=True)
                        nc.tensor.matmul(o[:, 0:D], w_hi, v[:, D + 2:VCOL], start=False, stop=False,
                                         skip_group_check=True)
                        last = nc.tensor.matmul(o, w_lo, v[:, 0:D + 1], start=False, stop=final and jj == 1,
                                                skip_group_check=True)
                    if final and u == 1:
                        last.then_inc(s_["o_half"], 1)
                last.then_inc(s_["pv_done"], 1)

            def turn_queries(n):
                pe.wait_ge(s_["hn_ready"], n + 1)
                wait(pe, "q_ready", n)
                for u in range(SUB):
                    last = nc.tensor.transpose(TQ[:, u * P:(u + 1) * P], hn1[:, u, :], ident[:, :])
                last.then_inc(s_["q_T"], 1)

            def run(layer, s, p, before):
                if before is None:
                    pe.wait_ge(s_["g_vlo"], 2 * NB)
                if layer == 1 and isinstance(s, int) and s == NB - 1:
                    pe.wait_ge(s_["q_ready"], s + 1)
                elif layer == 1:
                    pe.wait_ge(s_["moved"], s + 1)

                def step(it, kk, once):
                    k = UNROLL * it + kk
                    G = PAIRS * p + k
                    if layer == 0:
                        turn_adj(s, it, kk)
                    scores(layer, s, G, k, kk)
                    if not once or kk >= LAG:
                        products(layer, p, G - LAG, k - LAG, (kk - LAG) % UNROLL)
                    elif before is not None:
                        products(before, p - 1, G - LAG, PAIRS - LAG + kk, UNROLL - LAG + kk)

                pairs(pe, step)
                if before == 0:
                    turn_queries(block_before(layer, s, before))

            phases(pe, run)
            for kk in range(LAG):
                products(1, 2 * NB - 1, 2 * NB * PAIRS - LAG + kk, PAIRS - LAG + kk, UNROLL - LAG + kk)

        @block.scalar
        def _(act):
            act.wait_ge(s_["wT_ready"], 1)
            nc.scalar.activation(w_T[:, :], TQ[:, 0:P], ACT.Copy).then_inc(s_["w_ready"], 1)
            with act.Fori(0, NB // 2) as g2:
                for i in range(2):
                    g = 2 * g2 + i
                    act.wait_ge(s_["g_T"], 1 + g)
                    cols = bass.ds(g * BLK, BLK)
                    nc.scalar.activation(hT[i], S[i][:, 0:BLK], ACT.Copy).then_inc(s_["g_hT"], 1)
                    nc.scalar.activation(keys_hi[0][:, cols], S[i][:, 0:BLK], ACT.Copy).then_inc(s_["g_hi"], 1)
                    nc.scalar.activation(keys_hi[1][:, cols], S[i][:, BLK:2 * BLK], ACT.Copy).then_inc(
                        s_["g_hi"], 1)
                for i in range(2):
                    g = 2 * g2 + i
                    act.wait_ge(s_["g_v"], 1 + g)
                    for u in range(SUB):
                        last = nc.scalar.activation(vg[i][:, u, :], O[:, i, u * P:(u + 1) * P], ACT.Copy,
                                                    scale=col_g[i][:, 3, u:u + 1])
                    last.then_inc(s_["g_vs"], 1)
                    for u in range(SUB):
                        last = nc.scalar.activation(vals[0][:, bass.ds(g * SUB + u, 1), 0:D].rearrange("p a d -> p (a d)"),
                                                    O[:, i, u * P:(u + 1) * P], ACT.Copy,
                                                    scale=col_g[i][:, 3, u:u + 1])
                    last.then_inc(s_["g_vhi_x"], 1)

            def evacuate(layer, n, p):
                wait(act, "x1_ready" if layer == 0 else "res_ready", n)
                for half in range(2):
                    if half == 0:
                        act.wait_ge(s_["o_half"], p + 1)
                    else:
                        act.wait_ge(s_["pv_done"], PAIRS * (p + 1))
                    nc.scalar.activation(raw[layer][:, 2 * half:2 * half + 2, :],
                                         O[:, half, 0:2 * (D + 1)].rearrange("p (u c) -> p u c", u=2),
                                         ACT.Copy).then_inc(s_["o_free"], 1)

            def run(layer, s, p, before):
                def step(it, kk, once):
                    k = UNROLL * it + kk
                    G = PAIRS * p + k
                    if layer == 0:
                        act.wait_ge(s_["at_ready"], PAIRS * s + k + 1)
                        if not isinstance(s, int):
                            act.wait_ge(s_["wts_ready"], PAIRS * (p - 1) + k + 1)
                        nc.scalar.activation(mask_pair(s, k), AT[:, :].rearrange("p (t i) -> p t i", t=2),
                                             ACT.Copy).then_inc(s_["mask_ready"], 1)
                    act.wait_ge(s_["scores_ready"], G + 1)
                    wait(act, "wts_ready", G - 1)
                    e = expo[kk % 2][:, :]
                    if layer == 0:
                        nc.scalar.activation(e, S[kk % 2][:, :], ACT.Tanh, scale=tanh_scale[:, 0:1]).then_inc(
                            s_["scores_free"], 1)
                        act.wait_ge(s_["scores_free"], G + 1)
                        nc.scalar.activation(e, e, ACT.Exp, scale=8.0, bias=shift_col[:, 0:1]).then_inc(
                            s_["exp_ready"], 1)
                    else:
                        nc.scalar.activation(e, S[kk % 2][:, :], ACT.Exp, scale=COS).then_inc(
                            s_["scores_free"], 1)
                    if once and kk == LAG - 1 and before is not None:
                        evacuate(before, block_before(layer, s, before), p - 1)

                pairs(act, step)
                if before == 0:
                    n = block_before(layer, s, before)
                    act.wait_ge(s_["q_T"], n + 1)
                    wait(act, "moved", n)
                    nc.scalar.activation(q_next[:, 0, :], TQ[:, :], ACT.Copy).then_inc(s_["q_hi"], 1)

            act.wait_ge(s_["g_vhi_x"], NB)
            act.wait_ge(s_["g_vlo"], 2 * NB)
            act.wait_ge(s_["scale_ready"], 1)
            phases(act, run)
            evacuate(1, NB - 1, 2 * NB - 1)

        @block.vector
        def _(dve):
            with dve.Fori(0, NB // 2) as g2:
                for i in range(2):
                    g = 2 * g2 + i
                    dve.wait_ge(s_[f"x_loaded{i}"], 16 * (1 + g2))
                    for u in range(SUB):
                        last = nc.vector.bn_stats(stats_g[i][:, u, :], xg[i][:, u, :])
                    last.then_inc(s_["g_stats"], 1)
                for i in range(2):
                    g = 2 * g2 + i
                    dve.wait_ge(s_["g_stats"], g + 1)
                    dve.wait_ge(s_[f"y_loaded{i}"], 16 * (1 + g2))
                    for u in range(SUB):
                        last = nc.vector.tensor_tensor_reduce(out=yng[i][:, u, :], in0=yg[i][:, u, :],
                                                              in1=yg[i][:, u, :], scale=COS, scalar=0.0,
                                                              op0=ALU.mult, op1=ALU.add,
                                                              accum_out=col_g[i][:, 4, u:u + 1])
                    last.then_inc(s_["g_ssy_sum"], 1)
                    for u in range(SUB):
                        last = nc.vector.bn_aggr(mv_g[i][:, u, :], stats_g[i][:, u, :])
                    last.then_inc(s_["g_mv"], 1)
                for i in range(2):
                    dve.wait_ge(s_["g_ssy_sum"], 2 * g2 + i + 1)
                    nc.vector.tensor_scalar(col_g[i][:, 4, :], col_g[i][:, 4, :], NORM_EPS ** 2 * COS, None,
                                            ALU.max).then_inc(s_["g_ssy"], 1)
                for i in range(2):
                    g = 2 * g2 + i
                    dve.wait_ge(s_["g_rstd"], 1 + g)
                    for u in range(SUB):
                        last = nc.vector.tensor_scalar(hg[i][:, u, :], xg[i][:, u, :], mv_g[i][:, u, 0:1],
                                                       col_g[i][:, 0, u:u + 1], ALU.subtract, ALU.mult)
                    last.then_inc(s_["g_pre"], 1)
                for i in range(2):
                    dve.wait_ge(s_["g_pre"], 2 * g2 + i + 1)
                    nc.vector.tensor_scalar(hg[i], hg[i], 0.0, None, ALU.max).then_inc(s_["g_h"], 1)
                for i in range(2):
                    dve.wait_ge(s_["g_h"], 2 * g2 + i + 1)
                    for u in range(SUB):
                        last = nc.vector.tensor_tensor_reduce(out=hT[i][:, u * D:(u + 1) * D], in0=hg[i][:, u, :],
                                                              in1=hg[i][:, u, :], scale=COS, scalar=0.0,
                                                              op0=ALU.mult, op1=ALU.add,
                                                              accum_out=col_g[i][:, 1, u:u + 1])
                    last.then_inc(s_["g_ss"], 1)
                for i in range(2):
                    g = 2 * g2 + i
                    cols = bass.ds(g * BLK, BLK)
                    dve.wait_ge(s_["g_hi"], 2 * g + 2)
                    for l in range(2):
                        nc.vector.tensor_tensor(keys_lo[l][:, cols], S[i][:, l * BLK:(l + 1) * BLK],
                                                keys_hi[l][:, cols], ALU.subtract).then_inc(s_["g_lo"], 1)
                for i in range(2):
                    g = 2 * g2 + i
                    tiles = bass.ds(g * SUB, SUB)
                    dve.wait_ge(s_["g_vhi_x"], g + 1)
                    dve.wait_ge(s_["g_vhi_y"], g + 1)
                    nc.vector.tensor_tensor(vals[0][:, tiles, D + 2:VCOL], vg[i], vals[0][:, tiles, 0:D],
                                            ALU.subtract).then_inc(s_["g_vlo"], 1)
                    nc.vector.scalar_tensor_tensor(out=vals[1][:, tiles, D + 2:VCOL], in0=yg[i], scalar=VALUE,
                                                   in1=vals[1][:, tiles, 0:D], op0=ALU.mult,
                                                   op1=ALU.subtract).then_inc(s_["g_vlo"], 1)

            def hidden_a(n, p):
                dve.wait_ge(s_["o_free"], 2 * (p + 1))
                nc.vector.reciprocal(inv_sum[0][:, :], raw[0][:, :, D]).then_inc(s_["inv_sum_ready"], 1)
                dve.wait_ge(s_["inv_sum_ready"], n + 1)
                dve.wait_ge(s_["xres_ready"], n + 1)
                wait(dve, "base_ready", n)
                for u in range(SUB):
                    last = nc.vector.scalar_tensor_tensor(out=x1[:, u, :], in0=raw[0][:, u, 0:D],
                                                          scalar=inv_sum[0][:, u:u + 1], in1=x_res[:, u, :],
                                                          op0=ALU.mult, op1=ALU.add)
                last.then_inc(s_["x1_ready"], 1)
                dve.wait_ge(s_["x1_ready"], n + 1)
                for u in range(SUB):
                    last = nc.vector.bn_stats(stats[:, u, :], x1[:, u, :])
                last.then_inc(s_["stats_ready"], 1)

            def hidden_stats(n):
                for u in range(SUB):
                    last = nc.vector.bn_aggr(mv[:, u, :], stats[:, u, :])
                last.then_inc(s_["mv_ready"], 1)

            def hidden_b(n):
                dve.wait_ge(s_["rstd_ready"], n + 1)
                for u in range(SUB):
                    last = nc.vector.tensor_scalar(h1[:, u, :], x1[:, u, :], mv[:, u, 0:1], rstd[:, u:u + 1],
                                                   ALU.subtract, ALU.mult)
                last.then_inc(s_["hpre_ready"], 1)
                dve.wait_ge(s_["hpre_ready"], n + 1)
                nc.vector.tensor_scalar(h1[:, :, :], h1[:, :, :], 0.0, None, ALU.max).then_inc(s_["h_ready"], 1)
                dve.wait_ge(s_["h_ready"], n + 1)
                for u in range(SUB):
                    last = nc.vector.tensor_tensor_reduce(out=sq[:, u, :], in0=h1[:, u, :], in1=h1[:, u, :],
                                                          scale=COS, scalar=0.0, op0=ALU.mult, op1=ALU.add,
                                                          accum_out=ss[:, u:u + 1])
                last.then_inc(s_["ss_sum_ready"], 1)
                dve.wait_ge(s_["ss_sum_ready"], n + 1)
                nc.vector.tensor_scalar(ss[:, :], ss[:, :], NORM_EPS ** 2 * COS, None, ALU.max).then_inc(
                    s_["ss_ready"], 1)

            def finish(n, p):
                dve.wait_ge(s_["o_free"], 2 * (p + 1))
                nc.vector.reciprocal(inv_sum[1][:, :], raw[1][:, :, D]).then_inc(s_["inv_out_ready"], 1)
                dve.wait_ge(s_["inv_out_ready"], n + 1)
                nc.vector.tensor_scalar(inv_sum[1][:, :], inv_sum[1][:, :], 0.5, None, ALU.mult).then_inc(
                    s_["inv_half_ready"], 1)
                dve.wait_ge(s_["inv_half_ready"], n + 1)
                dve.wait_ge(s_["base_ready"], n + 1)
                wait(dve, "stored", 16 * n)
                for u in range(SUB):
                    last = nc.vector.scalar_tensor_tensor(out=res[:, u, :], in0=raw[1][:, u, 0:D],
                                                          scalar=inv_sum[1][:, u:u + 1], in1=base[:, u, :],
                                                          op0=ALU.mult, op1=ALU.add)
                last.then_inc(s_["res_ready"], 1)

            def run(layer, s, p, before):
                def step(it, kk, once):
                    k = UNROLL * it + kk
                    G = PAIRS * p + k
                    if layer == 0:
                        dve.wait_ge(s_["exp_ready"], PAIRS * s + k + 1)
                        dve.wait_ge(s_["mask_ready"], PAIRS * s + k + 1)
                    else:
                        dve.wait_ge(s_["scores_free"], G + 1)
                    wait(dve, "pv_done", G - UNROLL + 1)
                    hidden = once and before == 0
                    if hidden and kk == LAG + 1:
                        dve.wait_ge(s_["stats_ready"], block_before(layer, s, before) + 1)
                    w = wts[kk][:, :]
                    nc.vector.tensor_tensor(w.rearrange("p (t i) -> p t i", t=2),
                                            expo[kk % 2][:, :].rearrange("p (t i) -> p t i", t=2),
                                            mask_pair(s, k), ALU.mult).then_inc(s_["wts_ready"], 1)
                    if hidden and kk == LAG + 1:
                        hidden_stats(block_before(layer, s, before))
                    dve.wait_ge(s_["wts_ready"], G + 1)
                    hi = w.bitcast(BF16).rearrange("p (c two) -> p two c", two=2)[:, 1, :]
                    nc.vector.tensor_tensor(wts_lo[kk][:, :], w, hi, ALU.subtract).then_inc(s_["lo_ready"], 1)
                    if once and before is not None:
                        n = block_before(layer, s, before)
                        if before == 0 and kk == LAG:
                            hidden_a(n, p - 1)
                        if before == 0 and kk == LAG + 1:
                            hidden_b(n)
                        if before == 1 and kk == LAG:
                            finish(n, p - 1)

                pairs(dve, step)
                if before == 0:
                    dve.wait_ge(s_["q_hi"], block_before(layer, s, before) + 1)
                    nc.vector.tensor_tensor(q_next[:, 1, :], TQ[:, :], q_next[:, 0, :],
                                            ALU.subtract).then_inc(s_["q_ready"], 1)

            phases(dve, run)
            finish(NB - 1, 2 * NB - 1)

        @block.gpsimd
        def _(pool):
            nc.gpsimd.memset(ident[:, :], 0.0)
            nc.gpsimd.memset(ident_b[:, :], 0.0)
            nc.gpsimd.memset(neg_half[:, :], -0.5)
            nc.gpsimd.memset(pos_half[:, :], 0.5)
            nc.gpsimd.memset(eps_col[:, :], LN_EPS)
            nc.gpsimd.memset(value_col[:, :], VALUE)
            nc.gpsimd.memset(shift_col[:, :], LOG_SHIFT)
            for l in range(2):
                last = nc.gpsimd.memset(vals[l][:, :, D:D + 1], VALUE)
            last.then_inc(s_["zeros_ready"], 1)
            pool.wait_ge(s_["zeros_ready"], 1)
            for m in (ident, ident_b):
                last = nc.gpsimd.affine_select(out=m[:, :], in_=m[:, :], compare_op=ALU.not_equal, fill=1.0,
                                               base=0, pattern=[[-1, P]], channel_multiplier=1)
            last.then_inc(s_["idents_ready"], 1)
            pool.wait_ge(s_["const_loaded"], 48)
            nc.gpsimd.tensor_scalar(tanh_scale[:, :], b_col[:, :], COS / 8.0, 1.0, ALU.mult, ALU.mult).then_inc(
                s_["scale_ready"], 1)

            with pool.Fori(0, NB // 2) as g2:
                for i in range(2):
                    g = 2 * g2 + i
                    c = col_g[i]
                    pool.wait_ge(s_["g_mv"], 1 + g)
                    nc.gpsimd.tensor_tensor(c[:, 0, :], mv_g[i][:, :, 1], eps_col[:, :], ALU.add).then_inc(
                        s_["g_var"], 1)
                    pool.wait_ge(s_["g_var"], 1 + g)
                    nc.gpsimd.tensor_tensor(c[:, 0, :], c[:, 0, :], neg_half[:, :], ALU.pow).then_inc(
                        s_["g_rstd"], 1)
                for i in range(2):
                    g = 2 * g2 + i
                    c = col_g[i]
                    tiles = bass.ds(g * SUB, SUB)
                    pool.wait_ge(s_["g_ssy"], 1 + g)
                    nc.gpsimd.tensor_tensor(c[:, 5, :], c[:, 4, :], neg_half[:, :], ALU.pow).then_inc(
                        s_["g_invy"], 1)
                    pool.wait_ge(s_["g_invy"], 1 + g)
                    nc.gpsimd.tensor_tensor(yng[i], yg[i], c[:, 5, :].to_broadcast((P, SUB, D)), ALU.mult)
                    nc.gpsimd.tensor_tensor(vals[1][:, tiles, 0:D], yg[i],
                                            value_col[:, :].to_broadcast((P, SUB, D)),
                                            ALU.mult).then_inc(s_["g_vhi_y"], 1)
                for i in range(2):
                    g = 2 * g2 + i
                    c = col_g[i]
                    pool.wait_ge(s_["g_ss"], 1 + g)
                    nc.gpsimd.tensor_tensor(c[:, 2, :], c[:, 1, :], neg_half[:, :], ALU.pow).then_inc(
                        s_["g_inv"], 1)
                    nc.gpsimd.tensor_tensor(c[:, 3, :], c[:, 1, :], pos_half[:, :], ALU.pow).then_inc(
                        s_["g_inv"], 1)
                    pool.wait_ge(s_["g_inv"], 2 * g + 2)
                    nc.gpsimd.tensor_tensor(c[:, 3, :], c[:, 3, :], value_col[:, :].to_broadcast((P, SUB)),
                                            ALU.mult).then_inc(s_["g_norm"], 1)
                    nc.gpsimd.tensor_tensor(hg[i], hg[i], c[:, 2, :].to_broadcast((P, SUB, D)),
                                            ALU.mult).then_inc(s_["g_unit"], 1)

            def residual(n):
                pool.wait_ge(s_["xres_loaded"], 16 * (n + 1))
                for u in range(SUB):
                    last = nc.gpsimd.tensor_tensor(x_res[:, u, :], x_res[:, u, :], bias_row[:, :], ALU.add)
                last.then_inc(s_["xres_ready"], 1)

            def hidden(n):
                pool.wait_ge(s_["mv_ready"], n + 1)
                nc.gpsimd.tensor_tensor(rstd[:, :], mv[:, :, 1], eps_col[:, :], ALU.add).then_inc(
                    s_["var_ready"], 1)
                pool.wait_ge(s_["var_ready"], n + 1)
                nc.gpsimd.tensor_tensor(rstd[:, :], rstd[:, :], neg_half[:, :], ALU.pow).then_inc(
                    s_["rstd_ready"], 1)
                pool.wait_ge(s_["ss_ready"], n + 1)
                nc.gpsimd.tensor_tensor(inv[:, :], ss[:, :], neg_half[:, :], ALU.pow).then_inc(s_["inv_ready"], 1)
                wait(pool, "q_T", n)
                pool.wait_ge(s_["inv_ready"], n + 1)
                nc.gpsimd.tensor_tensor(hn1[:, :, :], h1[:, :, :], inv[:, :].to_broadcast((P, SUB, D)),
                                        ALU.mult).then_inc(s_["hn_ready"], 1)
                nc.gpsimd.tensor_tensor(half_h[:, :, :], h1[:, :, :], pos_half[:, 0:1].to_broadcast((P, SUB, D)),
                                        ALU.mult).then_inc(s_["half_ready"], 1)

            def residual_out(n):
                wait(pool, "res_ready", n)
                pool.wait_ge(s_["half_ready"], n + 1)
                nc.gpsimd.tensor_tensor(base[:, :, :], half_h[:, :, :], x1[:, :, :], ALU.add).then_inc(
                    s_["base_ready"], 1)

            def move(n, scores_done):
                wait(pool, "scores_ready", scores_done)
                pool.wait_ge(s_["q_ready"], n + 1)
                residual_out(n)
                nc.gpsimd.tensor_copy(q_now[:, :, :].rearrange("p a i -> p (a i)").bitcast(F32),
                                      q_next[:, :, :].rearrange("p a i -> p (a i)").bitcast(F32)).then_inc(
                    s_["moved"], 1)

            residual(0)
            hidden(0)
            move(0, 0)
            with pool.Fori(1, NB - 1) as n:
                residual(n)
                hidden(n)
                move(n, PAIRS * (2 * n + 1))
            residual(NB - 1)
            hidden(NB - 1)
            residual_out(NB - 1)


_INS = ['x', 'adj', 'L0_gnn_W', 'L0_gnn_bias', 'L0_gnn_b', 'L1_gnn_y']
_OUTS = [((4096, 128), 'float32')]


def kernel(**inputs):
    import numpy as _np
    import concourse.bacc as _bacc
    from concourse import mybir as _mybir
    from concourse.bass_utils import run_bass_kernel_spmd as _run

    nc = _bacc.Bacc("TRN2", target_bir_lowering=False, num_devices=1)
    arrays, args = {}, []
    for name in _INS:
        a = _np.ascontiguousarray(inputs[name])
        arrays[f"in_{name}_dram"] = a
        args.append(nc.dram_tensor(f"in_{name}_dram", a.shape, _mybir.dt.from_np(a.dtype), kind="ExternalInput").ap())
    for i, (shape, dtype) in enumerate(_OUTS):
        dt = _mybir.dt.from_np(_np.dtype(dtype))
        args.append(nc.dram_tensor(f"out_{i}_dram", shape, dt, kind="ExternalOutput").ap())
    two_layers(nc, *args)
    r = _run(nc, [arrays], core_ids=[0])
    return r.results[0]["out_0_dram"]
```

```python
from contextlib import ExitStack

import concourse.bass as bass
from concourse import mybir

F32 = mybir.dt.float32
F16 = mybir.dt.float16
BF16 = mybir.dt.bfloat16
ALU = mybir.AluOpType
ACT = mybir.ActivationFunctionType

P = 128
LN_EPS = 1e-5
NORM_EPS = 1e-8
UNIT = 64.0
VALUE = 16.0
COS = 1.0 / (UNIT * UNIT)
LOG_SHIFT = 11 * 0.6931471805599453


def two_layers(nc, x, adj, W, bias, b, y, out):
    N, D = x.shape
    NT = N // P
    SUB = 4
    BLK = SUB * P
    NB = N // BLK
    PAIRS = NT // 2
    UNROLL = 4
    ITERS = PAIRS // UNROLL
    CHUNK = 4 * P
    CHUNKS = N // CHUNK
    VCOL = 2 * D + 2
    LAG = 2
    assert D == P and PAIRS % UNROLL == 0

    with ExitStack() as ctx:
        def sb(name, shape, dt):
            return ctx.enter_context(nc.sbuf_tensor(name, shape, dt))

        def ps(name, shape, dt):
            return ctx.enter_context(nc.psum_tensor(name, shape, dt))

        def sem(name):
            return ctx.enter_context(nc.semaphore(name))

        keys_hi = [sb(f"keys_hi{l}", [P, N], F16) for l in range(2)]
        keys_lo = [sb(f"keys_lo{l}", [P, N], F16) for l in range(2)]
        vals = [sb(f"vals{l}", [P, NT, VCOL], F16) for l in range(2)]
        mask = sb("mask", [P, 2, NT, BLK], BF16)
        adj_in = [sb(f"adj_in{i}", [P, SUB, CHUNK], F32) for i in range(2)]
        expo = [sb(f"expo{i}", [P, 2 * BLK], F32) for i in range(2)]
        wts = [sb(f"wts{i}", [P, 2 * BLK], F32) for i in range(UNROLL)]
        wts_lo = [sb(f"wts_lo{i}", [P, 2 * BLK], F16) for i in range(UNROLL)]
        q_sb = sb("q_sb", [P, 2, BLK], F16)
        q_last = sb("q_last", [P, 2, BLK], F16)
        half_h = sb("half_h", [P, SUB, D], F32)
        base = sb("base", [P, SUB, D], F32)
        raw = [sb(f"raw{l}", [P, SUB, D + 1], F32) for l in range(2)]
        x_res = sb("x_res", [P, SUB, D], F32)
        x1 = sb("x1", [P, SUB, D], F32)
        h1 = sb("h1", [P, SUB, D], F32)
        hn1 = sb("hn1", [P, SUB, D], F32)
        res = sb("res", [P, SUB, D], F32)
        stats = sb("stats", [P, SUB, 6], F32)
        mv = sb("mv", [P, SUB, 2], F32)
        rstd = sb("rstd", [P, SUB], F32)
        ss = sb("ss", [P, SUB], F32)
        inv = sb("inv", [P, SUB], F32)
        inv_sum = [sb(f"inv_sum{l}", [P, SUB], F32) for l in range(2)]
        RING = 4
        hg = [wts[g // 2][:, g % 2 * BLK:(g % 2 + 1) * BLK].rearrange("p (u d) -> p u d", u=SUB)
              for g in range(NB)]
        hng = [wts_lo[g][:, :].bitcast(F32).rearrange("p (u d) -> p u d", u=SUB) for g in range(RING)]
        hT = [expo[g // 2][:, g % 2 * BLK:(g % 2 + 1) * BLK] for g in range(RING)]
        stats_g = [sb(f"stats_g{g}", [P, SUB, 6], F32) for g in range(NB)]
        mv_g = [sb(f"mv_g{g}", [P, SUB, 2], F32) for g in range(NB)]
        rstd_g = sb("rstd_g", [P, NB, SUB], F32)
        ss_g = sb("ss_g", [P, NB, SUB], F32)
        inv_g = sb("inv_g", [P, NB, SUB], F32)
        y_in = sb("y_in", [P, SUB, D], F32)
        y_big = res
        y_unit = sb("y_unit", [P, SUB, D], F32)
        ssy = sb("ssy", [P, SUB], F32)
        invy = sb("invy", [P, SUB], F32)
        w_in = sb("w_in", [P, D], F32)
        w_T = sb("w_T", [P, D], F32)
        bias_row = sb("bias_row", [P, D], F32)
        b_col = sb("b_col", [P, 1], F32)
        tanh_scale = sb("tanh_scale", [P, 1], F32)
        shift_col = sb("shift_col", [P, 1], F32)
        ident = sb("ident", [P, P], F32)
        ident_b = sb("ident_b", [P, P], BF16)
        neg_half = sb("neg_half", [P, SUB], F32)
        pos_half = sb("pos_half", [P, SUB], F32)
        eps_col = sb("eps_col", [P, SUB], F32)
        value_col = sb("value_col", [P, 1], F32)

        S = [ps(f"S{i}", [P, 2 * BLK], F32) for i in range(2)]
        O = ps("O", [P, 2, 512], F32)
        AT = ps("AT", [P, 2 * BLK], BF16)
        TQ = ps("TQ", [P, BLK], F32)
        hnT_ps = [S[0][:, 0:BLK], S[0][:, BLK:2 * BLK]]
        hT_ps = [S[1][:, 0:BLK], S[1][:, BLK:2 * BLK]]
        v_ps = [O[:, 0, :], O[:, 1, :]]

        names = """const_loaded zeros_ready idents_ready scale_ready wT_ready w_ready
            g_stats g_mv g_var g_rstd g_pre g_h g_ss g_inv g_unit g_T g_hi g_lo g_hT g_v g_vhi g_vlo
            y_loaded y_ss y_ss_max y_inv y_unit_ready y_T y_hi y_lo y_vhi y_vlo
            adj_loaded0 adj_loaded1 at_ready mask_ready scores_ready scores_free exp_ready
            wts_ready lo_ready pv_done o_half o_free
            xres_loaded xres_ready inv_sum_ready x1_ready stats_ready mv_ready var_ready rstd_ready hpre_ready
            h_ready ss_sum_ready ss_ready inv_ready hn_ready half_ready base_ready q_T q_hi q_ready
            inv_out_ready inv_half_ready res_ready stored""".split() + [f"x_loaded{g}" for g in range(NB)]
        s_ = {n: sem(n) for n in names}

        def wait(eng, name, value):
            if isinstance(value, int) and value <= 0:
                return
            eng.wait_ge(s_[name], value)

        adj_blocks = adj.rearrange("(s u p) j -> s p u j", u=SUB, p=P)
        x_blocks = x.rearrange("(s u p) d -> s p u d", u=SUB, p=P)
        y_blocks = y.rearrange("(s u p) d -> s p u d", u=SUB, p=P)
        out_blocks = out.rearrange("(s u p) d -> s p u d", u=SUB, p=P)

        def block_of(dram, s):
            return dram[bass.ds(s, 1)].rearrange("s p u d -> (s p) u d") if not isinstance(s, int) else dram[s]

        def phases(eng, run):
            run(0, 0, 0, None, None)
            run(0, 1, 1, 0, 0)
            run(1, 0, 2, 0, None)
            with eng.Fori(2, NB - 1) as s:
                run(0, s, 2 * s - 1, 1, s - 1)
                run(1, s - 1, 2 * s, 0, None)
            run(0, NB - 1, 2 * NB - 3, 1, NB - 2)
            run(1, NB - 2, 2 * NB - 2, 0, NB - 1)
            run(1, NB - 1, 2 * NB - 1, 1, None)

        def pairs(eng, step):
            for kk in range(UNROLL):
                step(0, kk, True, False)
            with eng.Fori(1, ITERS - 1) as it:
                for kk in range(UNROLL):
                    step(it, kk, False, False)
            for kk in range(UNROLL):
                step(ITERS - 1, kk, False, True)

        def mask_pair(s, k):
            first = (s % 2) * NT + 2 * k
            return mask[:, :, :, :].rearrange("p a t i -> p (a t) i")[:, bass.ds(first, 2), :]

        def with_y(p):
            return isinstance(p, int) and p < 2

        def block_before(layer, s, before):
            return {(0, 0): s - 1, (1, 0): s + 1, (0, 1): s - 2, (1, 1): s - 1}[(layer, before)]

        block = ctx.enter_context(nc.Block())

        @block.sync
        def _(sp):
            sp.dma_start(w_in[:, :], W).then_inc(s_["const_loaded"], 16)
            sp.dma_start(bias_row[:, :], bias.rearrange("(a d) -> a d", a=1).to_broadcast((P, D))).then_inc(
                s_["const_loaded"], 16)
            sp.dma_start(b_col[:, :], b.rearrange("(a d) -> a d", a=1).to_broadcast((P, 1))).then_inc(
                s_["const_loaded"], 16)

            for g in range(NB):
                sp.dma_start(hg[g], x_blocks[g]).then_inc(s_[f"x_loaded{g}"], 16)
            sp.dma_start(x_res[:, :, :], x_blocks[0]).then_inc(s_["xres_loaded"], 16)

            def load_y(g):
                wait(sp, "y_unit_ready", g)
                sp.dma_start(y_in[:, :, :], block_of(y_blocks, g)).then_inc(s_["y_loaded"], 16)

            def load_adj(s, c):
                wait(sp, "at_ready", 2 * (CHUNKS * s + c) - 2)
                sp.dma_start(adj_in[c % 2][:, :, :],
                             block_of(adj_blocks, s)[:, :, c * CHUNK:(c + 1) * CHUNK]).then_inc(
                    s_[f"adj_loaded{c % 2}"], 16)

            load_adj(0, 0)
            load_adj(0, 1)
            load_y(0)
            for n in range(2, 2 * CHUNKS):
                load_adj(n // CHUNKS, n % CHUNKS)
                if n % 2 == 1:
                    load_y(n // 2)
            with sp.Fori(2, NB) as s:
                for c in range(CHUNKS):
                    load_adj(s, c)

        @block.tensor
        def _(pe):
            pe.wait_ge(s_["idents_ready"], 1)
            pe.wait_ge(s_["const_loaded"], 48)
            nc.tensor.transpose(TQ[:, 0:P], w_in[:, :], ident[:, :]).then_inc(s_["wT_ready"], 1)

            def start_turn(g):
                pe.wait_ge(s_["g_unit"], 1 + g)
                wait(pe, "g_hi", g - 1)
                wait(pe, "g_lo", g - 1)
                for u in range(SUB):
                    nc.tensor.transpose(hnT_ps[g % 2][:, u * P:(u + 1) * P], hng[g % RING][:, u, :], ident[:, :])
                for u in range(SUB):
                    last = nc.tensor.transpose(hT_ps[g % 2][:, u * P:(u + 1) * P], hg[g][:, u, :], ident[:, :])
                last.then_inc(s_["g_T"], 1)

            def start_values(g):
                pe.wait_ge(s_["g_hT"], 1 + g)
                if g == 0:
                    pe.wait_ge(s_["w_ready"], 1)
                wait(pe, "g_vlo", g - 1)
                for u in range(SUB):
                    last = nc.tensor.matmul(v_ps[g % 2][:, u * P:(u + 1) * P], hT[g % RING][:, u * P:(u + 1) * P],
                                            w_T[:, :], start=True, stop=True)
                last.then_inc(s_["g_v"], 1)

            for t in range(NB + 1):
                if t < NB:
                    start_turn(t)
                if t >= 1:
                    start_values(t - 1)

            def turn_y(g):
                pe.wait_ge(s_["y_unit_ready"], g + 1)
                wait(pe, "y_lo", g)
                if isinstance(g, int) and g == NB - 1:
                    pe.wait_ge(s_["q_ready"], 1)
                for u in range(SUB):
                    last = nc.tensor.transpose(TQ[:, u * P:(u + 1) * P], y_unit[:, u, :], ident[:, :])
                last.then_inc(s_["y_T"], 1)

            def scores(layer, s, G, k, kk):
                wait(pe, "scores_free", G - 1)
                dst = S[kk % 2]
                for jj in range(2):
                    cols = bass.ds((2 * k + jj) * P, P)
                    k_hi, k_lo = keys_hi[layer][:, cols], keys_lo[layer][:, cols]
                    if layer == 0:
                        q_hi = keys_hi[0][:, bass.ds(s * BLK, BLK)]
                        q_lo = keys_lo[0][:, bass.ds(s * BLK, BLK)]
                    else:
                        q = q_last if isinstance(s, int) and s == NB - 1 else q_sb
                        q_hi, q_lo = q[:, 0, :], q[:, 1, :]
                    o = dst[:, jj * BLK:(jj + 1) * BLK]
                    nc.tensor.matmul(o, k_hi, q_hi, start=True, stop=False)
                    nc.tensor.matmul(o, k_hi, q_lo, start=False, stop=False)
                    last = nc.tensor.matmul(o, k_lo, q_hi, start=False, stop=True)
                last.then_inc(s_["scores_ready"], 1)

            def turn_adj(s, it, kk):
                if kk % 2 == 0:
                    pe.wait_ge(s_[f"adj_loaded{kk // 2}"], 16 * (ITERS * s + it + 1))
                wait(pe, "mask_ready", PAIRS * s + UNROLL * it + kk)
                src = adj_in[kk // 2][:, :, :].bitcast(BF16).rearrange("p u (j two) -> p u two j", two=2)
                for jj in range(2):
                    for u in range(SUB):
                        c0 = (2 * (kk % 2) + jj) * P
                        last = nc.tensor.transpose(AT[:, (jj * SUB + u) * P:(jj * SUB + u + 1) * P],
                                                   src[:, u, 1, c0:c0 + P], ident_b[:, :])
                last.then_inc(s_["at_ready"], 1)

            def products(layer, p, G, k, slot):
                first = isinstance(k, int) and k == 0
                final = isinstance(k, int) and k == PAIRS - 1
                if first:
                    wait(pe, "o_free", 2 * p)
                pe.wait_ge(s_["lo_ready"], G + 1)
                hi = wts[slot][:, :].bitcast(BF16).rearrange("p (c two) -> p two c", two=2)
                for u in range(SUB):
                    o = O[:, u // 2, (u % 2) * (D + 1):(u % 2 + 1) * (D + 1)]
                    for jj in range(2):
                        c0 = jj * BLK + u * P
                        tile = 2 * k + jj
                        if isinstance(k, int):
                            v = vals[layer][:, tile, :]
                        else:
                            v = vals[layer][:, bass.ds(tile, 1), :].rearrange("p a c -> p (a c)")
                        w_hi, w_lo = hi[:, 1, c0:c0 + P], wts_lo[slot][:, c0:c0 + P]
                        nc.tensor.matmul(o, w_hi, v[:, 0:D + 1], start=first and jj == 0 and u % 2 == 0,
                                         stop=False, skip_group_check=True)
                        nc.tensor.matmul(o[:, 0:D], w_hi, v[:, D + 2:VCOL], start=False, stop=False,
                                         skip_group_check=True)
                        last = nc.tensor.matmul(o, w_lo, v[:, 0:D + 1], start=False, stop=final and jj == 1,
                                                skip_group_check=True)
                    if final and u == 1:
                        last.then_inc(s_["o_half"], 1)
                last.then_inc(s_["pv_done"], 1)

            def turn_queries(n):
                pe.wait_ge(s_["hn_ready"], n + 1)
                pe.wait_ge(s_["y_lo"], NB - 1 if isinstance(n, int) and n == 0 else NB)
                wait(pe, "q_ready", n)
                for u in range(SUB):
                    last = nc.tensor.transpose(TQ[:, u * P:(u + 1) * P], hn1[:, u, :], ident[:, :])
                last.then_inc(s_["q_T"], 1)

            def run(layer, s, p, before, hidden):
                if before is None:
                    pe.wait_ge(s_["g_vlo"], NB)
                if layer == 1:
                    pe.wait_ge(s_["q_ready"], s + 1)
                if isinstance(p, int) and p == 2:
                    pe.wait_ge(s_["y_vlo"], NB)

                def step(it, kk, first, last):
                    k = UNROLL * it + kk
                    G = PAIRS * p + k
                    if with_y(p) and kk == UNROLL - 1:
                        turn_y(ITERS * p + it)
                    if hidden is not None and last and kk == 0:
                        turn_queries(hidden)
                    if layer == 0:
                        turn_adj(s, it, kk)
                    scores(layer, s, G, k, kk)
                    if not first or kk >= LAG:
                        products(layer, p, G - LAG, k - LAG, (kk - LAG) % UNROLL)
                    elif before is not None:
                        products(before, p - 1, G - LAG, PAIRS - LAG + kk, UNROLL - LAG + kk)

                pairs(pe, step)

            phases(pe, run)
            for kk in range(LAG):
                products(1, 2 * NB - 1, 2 * NB * PAIRS - LAG + kk, PAIRS - LAG + kk, UNROLL - LAG + kk)

        @block.scalar
        def _(act):
            act.wait_ge(s_["wT_ready"], 1)
            nc.scalar.activation(w_T[:, :], TQ[:, 0:P], ACT.Copy, scale=VALUE).then_inc(s_["w_ready"], 1)

            def start_h(g):
                act.wait_ge(s_["g_pre"], g + 1)
                nc.scalar.activation(hg[g], hg[g], ACT.Relu).then_inc(s_["g_h"], 1)
                act.wait_ge(s_["g_h"], g + 1)
                wait(act, "g_T", g - RING + 1)
                for u in range(SUB):
                    last = nc.scalar.activation(hng[g % RING][:, u, :], hg[g][:, u, :], ACT.Square,
                                                scale=1.0 / UNIT, accum_out=ss_g[:, g, u:u + 1])
                last.then_inc(s_["g_ss"], 1)

            def start_keys(g):
                act.wait_ge(s_["g_T"], g + 1)
                wait(act, "g_v", g - RING + 1)
                nc.scalar.activation(hT[g % RING], hT_ps[g % 2], ACT.Copy).then_inc(s_["g_hT"], 1)
                nc.scalar.activation(keys_hi[0][:, g * BLK:(g + 1) * BLK], hnT_ps[g % 2], ACT.Copy).then_inc(
                    s_["g_hi"], 1)

            def start_values(g):
                act.wait_ge(s_["g_v"], g + 1)
                nc.scalar.activation(vals[0][:, g * SUB:(g + 1) * SUB, 0:D],
                                     v_ps[g % 2].rearrange("p (u d) -> p u d", u=SUB), ACT.Copy).then_inc(
                    s_["g_vhi"], 1)

            for t in range(NB + 2):
                if t < NB:
                    start_h(t)
                if 1 <= t <= NB:
                    start_keys(t - 1)
                if t >= 2:
                    start_values(t - 2)

            def y_squares(g):
                act.wait_ge(s_["y_loaded"], 16 * (g + 1))
                wait(act, "y_T", g)
                for u in range(SUB):
                    last = nc.scalar.activation(y_unit[:, u, :], y_in[:, u, :], ACT.Square, scale=1.0 / UNIT,
                                                accum_out=ssy[:, u:u + 1])
                last.then_inc(s_["y_ss"], 1)

            def store(n):
                act.wait_ge(s_["res_ready"], n + 1)
                act.dma_start(block_of(out_blocks, n), res[:, :, :]).then_inc(s_["stored"], 16)

            def evacuate(layer, n, p):
                wait(act, "x1_ready" if layer == 0 else "res_ready", n)
                for half in range(2):
                    if half == 0:
                        act.wait_ge(s_["o_half"], p + 1)
                    else:
                        act.wait_ge(s_["pv_done"], PAIRS * (p + 1))
                    nc.scalar.activation(raw[layer][:, 2 * half:2 * half + 2, :],
                                         O[:, half, 0:2 * (D + 1)].rearrange("p (u c) -> p u c", u=2),
                                         ACT.Copy).then_inc(s_["o_free"], 1)

            def run(layer, s, p, before, hidden):
                def step(it, kk, first, last):
                    k = UNROLL * it + kk
                    G = PAIRS * p + k
                    if with_y(p) and kk == 0:
                        y_squares(ITERS * p + it)
                    if layer == 0:
                        act.wait_ge(s_["at_ready"], PAIRS * s + k + 1)
                        if not (isinstance(s, int) and s < 2):
                            act.wait_ge(s_["wts_ready"], PAIRS * (p - 1) + k + 1)
                        nc.scalar.activation(mask_pair(s, k), AT[:, :].rearrange("p (t i) -> p t i", t=2),
                                             ACT.Copy).then_inc(s_["mask_ready"], 1)
                    act.wait_ge(s_["scores_ready"], G + 1)
                    wait(act, "wts_ready", G - 1)
                    e = expo[kk % 2][:, :]
                    if layer == 0:
                        nc.scalar.activation(e, S[kk % 2][:, :], ACT.Tanh, scale=tanh_scale[:, 0:1]).then_inc(
                            s_["scores_free"], 1)
                        act.wait_ge(s_["scores_free"], G + 1)
                        nc.scalar.activation(e, e, ACT.Exp, scale=8.0, bias=shift_col[:, 0:1]).then_inc(
                            s_["exp_ready"], 1)
                    else:
                        nc.scalar.activation(e, S[kk % 2][:, :], ACT.Exp, scale=COS).then_inc(
                            s_["scores_free"], 1)
                    if first and kk == LAG - 1 and before is not None:
                        evacuate(before, block_before(layer, s, before), p - 1)
                    if with_y(p) and kk == UNROLL - 1:
                        g = ITERS * p + it
                        act.wait_ge(s_["y_T"], g + 1)
                        nc.scalar.activation(keys_hi[1][:, bass.ds(g * BLK, BLK)], TQ[:, :], ACT.Copy).then_inc(
                            s_["y_hi"], 1)
                    if hidden is not None and last and kk == 0:
                        act.wait_ge(s_["q_T"], hidden + 1)
                        q = q_last if isinstance(hidden, int) and hidden == NB - 1 else q_sb
                        nc.scalar.activation(q[:, 0, :], TQ[:, :], ACT.Copy).then_inc(s_["q_hi"], 1)

                pairs(act, step)
                if layer == 0 and not (isinstance(s, int) and s == 0):
                    act.wait_ge(s_["x1_ready"], s)
                    act.dma_start(x_res[:, :, :], block_of(x_blocks, s)).then_inc(s_["xres_loaded"], 16)
                if before == 1:
                    store(block_before(layer, s, before))

            act.wait_ge(s_["g_vlo"], NB)
            act.wait_ge(s_["scale_ready"], 1)
            phases(act, run)
            evacuate(1, NB - 1, 2 * NB - 1)
            store(NB - 1)
            act.wait_ge(s_["stored"], 16 * NB)

        @block.vector
        def _(dve):
            def start_stats(g):
                dve.wait_ge(s_[f"x_loaded{g}"], 16)
                for u in range(SUB):
                    last = nc.vector.bn_stats(stats_g[g][:, u, :], hg[g][:, u, :])
                last.then_inc(s_["g_stats"], 1)

            def start_mv(g):
                dve.wait_ge(s_["g_stats"], g + 1)
                for u in range(SUB):
                    last = nc.vector.bn_aggr(mv_g[g][:, u, :], stats_g[g][:, u, :])
                last.then_inc(s_["g_mv"], 1)

            def start_norm(g):
                dve.wait_ge(s_["g_rstd"], g + 1)
                for u in range(SUB):
                    last = nc.vector.tensor_scalar(hg[g][:, u, :], hg[g][:, u, :], mv_g[g][:, u, 0:1],
                                                   rstd_g[:, g, u:u + 1], ALU.subtract, ALU.mult)
                last.then_inc(s_["g_pre"], 1)

            def start_keys(g):
                dve.wait_ge(s_["g_hi"], g + 1)
                cols = slice(g * BLK, (g + 1) * BLK)
                nc.vector.tensor_tensor(keys_lo[0][:, cols], hnT_ps[g % 2], keys_hi[0][:, cols],
                                        ALU.subtract).then_inc(s_["g_lo"], 1)

            def start_values(g):
                dve.wait_ge(s_["g_vhi"], g + 1)
                tiles = slice(g * SUB, (g + 1) * SUB)
                nc.vector.tensor_tensor(vals[0][:, tiles, D + 2:VCOL],
                                        v_ps[g % 2].rearrange("p (u d) -> p u d", u=SUB),
                                        vals[0][:, tiles, 0:D], ALU.subtract).then_inc(s_["g_vlo"], 1)

            start_stats(0)
            for t in range(NB + 4):
                if t + 1 < NB:
                    start_stats(t + 1)
                if t < NB:
                    start_mv(t)
                if 1 <= t <= NB:
                    start_norm(t - 1)
                if 3 <= t < NB + 3:
                    start_keys(t - 3)
                if t >= 4:
                    start_values(t - 4)

            def y_low(g):
                dve.wait_ge(s_["y_vhi"], g + 1)
                tiles = bass.ds(g * SUB, SUB)
                nc.vector.tensor_tensor(vals[1][:, tiles, D + 2:VCOL], y_big[:, :, :], vals[1][:, tiles, 0:D],
                                        ALU.subtract).then_inc(s_["y_vlo"], 1)
                dve.wait_ge(s_["y_hi"], g + 1)
                cols = bass.ds(g * BLK, BLK)
                nc.vector.tensor_tensor(keys_lo[1][:, cols], TQ[:, :], keys_hi[1][:, cols],
                                        ALU.subtract).then_inc(s_["y_lo"], 1)

            def hidden_a(n, p):
                dve.wait_ge(s_["o_free"], 2 * (p + 1))
                nc.vector.reciprocal(inv_sum[0][:, :], raw[0][:, :, D]).then_inc(s_["inv_sum_ready"], 1)
                dve.wait_ge(s_["inv_sum_ready"], n + 1)
                dve.wait_ge(s_["xres_ready"], n + 1)
                wait(dve, "base_ready", n)
                for u in range(SUB):
                    last = nc.vector.scalar_tensor_tensor(out=x1[:, u, :], in0=raw[0][:, u, 0:D],
                                                          scalar=inv_sum[0][:, u:u + 1], in1=x_res[:, u, :],
                                                          op0=ALU.mult, op1=ALU.add)
                last.then_inc(s_["x1_ready"], 1)
                dve.wait_ge(s_["x1_ready"], n + 1)
                for u in range(SUB):
                    last = nc.vector.bn_stats(stats[:, u, :], x1[:, u, :])
                last.then_inc(s_["stats_ready"], 1)

            def hidden_stats(n):
                for u in range(SUB):
                    last = nc.vector.bn_aggr(mv[:, u, :], stats[:, u, :])
                last.then_inc(s_["mv_ready"], 1)

            def hidden_b(n):
                dve.wait_ge(s_["rstd_ready"], n + 1)
                for u in range(SUB):
                    last = nc.vector.tensor_scalar(h1[:, u, :], x1[:, u, :], mv[:, u, 0:1], rstd[:, u:u + 1],
                                                   ALU.subtract, ALU.mult)
                last.then_inc(s_["hpre_ready"], 1)
                dve.wait_ge(s_["hpre_ready"], n + 1)
                nc.vector.tensor_scalar(h1[:, :, :], h1[:, :, :], 0.0, None, ALU.max).then_inc(s_["h_ready"], 1)
                dve.wait_ge(s_["h_ready"], n + 1)
                for u in range(SUB):
                    last = nc.vector.tensor_tensor_reduce(out=hn1[:, u, :], in0=h1[:, u, :], in1=h1[:, u, :],
                                                          scale=COS, scalar=0.0, op0=ALU.mult, op1=ALU.add,
                                                          accum_out=ss[:, u:u + 1])
                last.then_inc(s_["ss_sum_ready"], 1)
                dve.wait_ge(s_["ss_sum_ready"], n + 1)
                nc.vector.tensor_scalar(ss[:, :], ss[:, :], NORM_EPS ** 2 * COS, None, ALU.max).then_inc(
                    s_["ss_ready"], 1)

            def finish(n, p):
                dve.wait_ge(s_["o_free"], 2 * (p + 1))
                nc.vector.reciprocal(inv_sum[1][:, :], raw[1][:, :, D]).then_inc(s_["inv_out_ready"], 1)
                dve.wait_ge(s_["inv_out_ready"], n + 1)
                nc.vector.tensor_scalar(inv_sum[1][:, :], inv_sum[1][:, :], 0.5, None, ALU.mult).then_inc(
                    s_["inv_half_ready"], 1)
                dve.wait_ge(s_["inv_half_ready"], n + 1)
                dve.wait_ge(s_["base_ready"], n + 1)
                wait(dve, "stored", 16 * n)
                for u in range(SUB):
                    last = nc.vector.scalar_tensor_tensor(out=res[:, u, :], in0=raw[1][:, u, 0:D],
                                                          scalar=inv_sum[1][:, u:u + 1], in1=base[:, u, :],
                                                          op0=ALU.mult, op1=ALU.add)
                last.then_inc(s_["res_ready"], 1)

            def run(layer, s, p, before, hidden):
                at = 0 if before == 1 else LAG
                p_sums = p - 1 if before == 0 else p - 2

                def step(it, kk, first, last):
                    k = UNROLL * it + kk
                    G = PAIRS * p + k
                    if layer == 0:
                        dve.wait_ge(s_["exp_ready"], PAIRS * s + k + 1)
                        dve.wait_ge(s_["mask_ready"], PAIRS * s + k + 1)
                    else:
                        dve.wait_ge(s_["scores_free"], G + 1)
                    wait(dve, "pv_done", G - UNROLL + 1)
                    w = wts[kk][:, :]
                    now = first and hidden is not None
                    if now and kk == at + 1:
                        dve.wait_ge(s_["stats_ready"], hidden + 1)
                    nc.vector.tensor_tensor(w.rearrange("p (t i) -> p t i", t=2),
                                            expo[kk % 2][:, :].rearrange("p (t i) -> p t i", t=2),
                                            mask_pair(s, k), ALU.mult).then_inc(s_["wts_ready"], 1)
                    if now and kk == at + 1:
                        hidden_stats(hidden)
                    dve.wait_ge(s_["wts_ready"], G + 1)
                    hi = w.bitcast(BF16).rearrange("p (c two) -> p two c", two=2)[:, 1, :]
                    nc.vector.tensor_tensor(wts_lo[kk][:, :], w, hi, ALU.subtract).then_inc(s_["lo_ready"], 1)
                    if now and kk == at:
                        hidden_a(hidden, p_sums)
                    if now and kk == UNROLL - 1:
                        hidden_b(hidden)
                    if first and before == 1 and kk == LAG:
                        finish(block_before(layer, s, before), p - 1)
                    if with_y(p) and kk == UNROLL - 1:
                        y_low(ITERS * p + it)
                    if hidden is not None and last and kk == 0:
                        dve.wait_ge(s_["q_hi"], hidden + 1)
                        q = q_last if isinstance(hidden, int) and hidden == NB - 1 else q_sb
                        nc.vector.tensor_tensor(q[:, 1, :], TQ[:, :], q[:, 0, :],
                                                ALU.subtract).then_inc(s_["q_ready"], 1)

                pairs(dve, step)

            phases(dve, run)
            finish(NB - 1, 2 * NB - 1)

        @block.gpsimd
        def _(pool):
            nc.gpsimd.memset(ident[:, :], 0.0)
            nc.gpsimd.memset(ident_b[:, :], 0.0)
            nc.gpsimd.memset(neg_half[:, :], -0.5)
            nc.gpsimd.memset(pos_half[:, :], 0.5)
            nc.gpsimd.memset(eps_col[:, :], LN_EPS)
            nc.gpsimd.memset(value_col[:, :], VALUE)
            nc.gpsimd.memset(shift_col[:, :], LOG_SHIFT)
            for l in range(2):
                last = nc.gpsimd.memset(vals[l][:, :, D:D + 1], VALUE)
            last.then_inc(s_["zeros_ready"], 1)
            pool.wait_ge(s_["zeros_ready"], 1)
            for m in (ident, ident_b):
                last = nc.gpsimd.affine_select(out=m[:, :], in_=m[:, :], compare_op=ALU.not_equal, fill=1.0,
                                               base=0, pattern=[[-1, P]], channel_multiplier=1)
            last.then_inc(s_["idents_ready"], 1)
            pool.wait_ge(s_["const_loaded"], 48)
            nc.gpsimd.tensor_scalar(tanh_scale[:, :], b_col[:, :], COS / 8.0, 1.0, ALU.mult, ALU.mult).then_inc(
                s_["scale_ready"], 1)

            def start_rstd(g):
                pool.wait_ge(s_["g_mv"], g + 1)
                nc.gpsimd.tensor_tensor(rstd_g[:, g, :], mv_g[g][:, :, 1], eps_col[:, :], ALU.add).then_inc(
                    s_["g_var"], 1)
                pool.wait_ge(s_["g_var"], g + 1)
                nc.gpsimd.tensor_tensor(rstd_g[:, g, :], rstd_g[:, g, :], neg_half[:, :], ALU.pow).then_inc(
                    s_["g_rstd"], 1)

            def start_unit(g):
                pool.wait_ge(s_["g_ss"], g + 1)
                nc.gpsimd.tensor_tensor(inv_g[:, g, :], ss_g[:, g, :], neg_half[:, :], ALU.pow).then_inc(
                    s_["g_inv"], 1)
                pool.wait_ge(s_["g_inv"], g + 1)
                nc.gpsimd.tensor_tensor(hng[g % RING], hg[g], inv_g[:, g, :].to_broadcast((P, SUB, D)),
                                        ALU.mult).then_inc(s_["g_unit"], 1)

            for t in range(NB + 1):
                if t < NB:
                    start_rstd(t)
                if t >= 1:
                    start_unit(t - 1)

            def y_group(g):
                pool.wait_ge(s_["y_ss"], g + 1)
                wait(pool, "y_vlo", g)
                nc.gpsimd.tensor_tensor(y_big[:, :, :], y_in[:, :, :], value_col[:, :].to_broadcast((P, SUB, D)),
                                        ALU.mult)
                nc.gpsimd.tensor_scalar(ssy[:, :], ssy[:, :], NORM_EPS ** 2 * COS, 3e38, ALU.max,
                                        ALU.min).then_inc(s_["y_ss_max"], 1)
                pool.wait_ge(s_["y_ss_max"], g + 1)
                nc.gpsimd.tensor_tensor(invy[:, :], ssy[:, :], neg_half[:, :], ALU.pow).then_inc(s_["y_inv"], 1)
                pool.wait_ge(s_["y_inv"], g + 1)
                nc.gpsimd.tensor_tensor(y_unit[:, :, :], y_in[:, :, :], invy[:, :].to_broadcast((P, SUB, D)),
                                        ALU.mult).then_inc(s_["y_unit_ready"], 1)
                nc.gpsimd.tensor_copy(vals[1][:, bass.ds(g * SUB, SUB), 0:D], y_big[:, :, :]).then_inc(
                    s_["y_vhi"], 1)

            y_group(0)
            with pool.Fori(1, ITERS) as g:
                y_group(g)

            def residual(n):
                pool.wait_ge(s_["xres_loaded"], 16 * (n + 1))
                for u in range(SUB):
                    last = nc.gpsimd.tensor_tensor(x_res[:, u, :], x_res[:, u, :], bias_row[:, :], ALU.add)
                last.then_inc(s_["xres_ready"], 1)

            def hidden(n):
                pool.wait_ge(s_["mv_ready"], n + 1)
                nc.gpsimd.tensor_tensor(rstd[:, :], mv[:, :, 1], eps_col[:, :], ALU.add).then_inc(
                    s_["var_ready"], 1)
                pool.wait_ge(s_["var_ready"], n + 1)
                nc.gpsimd.tensor_tensor(rstd[:, :], rstd[:, :], neg_half[:, :], ALU.pow).then_inc(
                    s_["rstd_ready"], 1)
                pool.wait_ge(s_["ss_ready"], n + 1)
                nc.gpsimd.tensor_tensor(inv[:, :], ss[:, :], neg_half[:, :], ALU.pow).then_inc(s_["inv_ready"], 1)
                wait(pool, "q_T", n)
                pool.wait_ge(s_["inv_ready"], n + 1)
                nc.gpsimd.tensor_tensor(hn1[:, :, :], h1[:, :, :], inv[:, :].to_broadcast((P, SUB, D)),
                                        ALU.mult).then_inc(s_["hn_ready"], 1)
                nc.gpsimd.tensor_tensor(half_h[:, :, :], h1[:, :, :], pos_half[:, 0:1].to_broadcast((P, SUB, D)),
                                        ALU.mult).then_inc(s_["half_ready"], 1)

            def residual_out(n):
                wait(pool, "res_ready", n)
                pool.wait_ge(s_["half_ready"], n + 1)
                nc.gpsimd.tensor_tensor(base[:, :, :], half_h[:, :, :], x1[:, :, :], ALU.add).then_inc(
                    s_["base_ready"], 1)

            residual(0)
            y_group(ITERS)
            hidden(0)
            residual_out(0)
            with pool.Fori(ITERS + 1, 2 * ITERS) as g:
                y_group(g)
            with pool.Fori(1, NB) as n:
                residual(n)
                hidden(n)
                residual_out(n)


_INS = ['x', 'adj', 'L0_gnn_W', 'L0_gnn_bias', 'L0_gnn_b', 'L1_gnn_y']
_OUTS = [((4096, 128), 'float32')]


def kernel(**inputs):
    import numpy as _np
    import concourse.bacc as _bacc
    from concourse import mybir as _mybir
    from concourse.bass_utils import run_bass_kernel_spmd as _run

    nc = _bacc.Bacc("TRN2", target_bir_lowering=False, num_devices=1)
    arrays, args = {}, []
    for name in _INS:
        a = _np.ascontiguousarray(inputs[name])
        arrays[f"in_{name}_dram"] = a
        args.append(nc.dram_tensor(f"in_{name}_dram", a.shape, _mybir.dt.from_np(a.dtype), kind="ExternalInput").ap())
    for i, (shape, dtype) in enumerate(_OUTS):
        dt = _mybir.dt.from_np(_np.dtype(dtype))
        args.append(nc.dram_tensor(f"out_{i}_dram", shape, dt, kind="ExternalOutput").ap())
    two_layers(nc, *args)
    r = _run(nc, [arrays], core_ids=[0])
    return r.results[0]["out_0_dram"]
```

```python
from contextlib import ExitStack

import concourse.bass as bass
from concourse import mybir

F32 = mybir.dt.float32
F16 = mybir.dt.float16
BF16 = mybir.dt.bfloat16
ALU = mybir.AluOpType
ACT = mybir.ActivationFunctionType

P = 128
LN_EPS = 1e-5
NORM_EPS = 1e-8
UNIT = 64.0
VALUE = 16.0
COS = 1.0 / (UNIT * UNIT)
LOG_SHIFT = 11 * 0.6931471805599453


def two_layers(nc, x, adj, W, bias, b, y, out):
    N, D = x.shape
    NT = N // P
    SUB = 4
    BLK = SUB * P
    NB = N // BLK
    PAIRS = NT // 2
    UNROLL = 4
    ITERS = PAIRS // UNROLL
    CHUNK = 4 * P
    CHUNKS = N // CHUNK
    VCOL = 2 * D + 2
    YAHEAD = 5
    LAG = 3
    assert D == P and PAIRS % UNROLL == 0

    with ExitStack() as ctx:
        def sb(name, shape, dt):
            return ctx.enter_context(nc.sbuf_tensor(name, shape, dt))

        def ps(name, shape, dt):
            return ctx.enter_context(nc.psum_tensor(name, shape, dt))

        def sem(name):
            return ctx.enter_context(nc.semaphore(name))

        keys_hi = [sb(f"keys_hi{l}", [P, N], F16) for l in range(2)]
        keys_lo = [sb(f"keys_lo{l}", [P, N], F16) for l in range(2)]
        vals = [sb(f"vals{l}", [P, NT, VCOL], F16) for l in range(2)]
        mask = sb("mask", [P, 2, NT, BLK], BF16)
        adj_in = [sb(f"adj_in{i}", [P, SUB, CHUNK], F32) for i in range(2)]
        wts = [sb(f"wts{i}", [P, 2 * BLK], F32) for i in range(UNROLL)]
        wts_lo = [sb(f"wts_lo{i}", [P, 2 * BLK], F16) for i in range(UNROLL)]
        q_sb = sb("q_sb", [P, 2, BLK], F16)
        q_last = sb("q_last", [P, 2, BLK], F16)
        half_h = sb("half_h", [P, SUB, D], F32)
        base = sb("base", [P, SUB, D], F32)
        raw = [sb(f"raw{l}", [P, SUB, D + 1], F32) for l in range(2)]
        x_res = sb("x_res", [P, SUB, D], F32)
        x1 = sb("x1", [P, SUB, D], F32)
        h1 = sb("h1", [P, SUB, D], F32)
        hn1 = sb("hn1", [P, SUB, D], F32)
        res = sb("res", [P, SUB, D], F32)
        stats = sb("stats", [P, SUB, 6], F32)
        mv = sb("mv", [P, SUB, 2], F32)
        rstd = sb("rstd", [P, SUB], F32)
        ss = sb("ss", [P, SUB], F32)
        inv = sb("inv", [P, SUB], F32)
        inv_sum = [sb(f"inv_sum{l}", [P, SUB], F32) for l in range(2)]
        RING = 4
        hg = [wts[g // 2][:, g % 2 * BLK:(g % 2 + 1) * BLK].rearrange("p (u d) -> p u d", u=SUB)
              for g in range(NB)]
        hng = [wts_lo[g][:, :].bitcast(F32).rearrange("p (u d) -> p u d", u=SUB) for g in range(RING)]
        hT = [mask[:, 1, 2 * g:2 * g + 2, :].rearrange("p t i -> p (t i)").bitcast(F32) for g in range(RING)]
        stats_g = [sb(f"stats_g{g}", [P, SUB, 6], F32) for g in range(NB)]
        mv_g = [sb(f"mv_g{g}", [P, SUB, 2], F32) for g in range(NB)]
        rstd_g = sb("rstd_g", [P, NB, SUB], F32)
        ss_g = sb("ss_g", [P, NB, SUB], F32)
        inv_g = sb("inv_g", [P, NB, SUB], F32)
        y_in0 = sb("y_in0", [P, SUB, D], F32)
        y_in = [y_in0[:, :, :], raw[1][:, :, 0:D]]
        y_big = res
        y_unit = sb("y_unit", [P, SUB, D], F32)
        packed = [buffer[:, :, :].bitcast(BF16) for buffer in (y_in0, y_unit)]
        ssy = sb("ssy", [P, SUB], F32)
        invy = sb("invy", [P, SUB], F32)
        w_in = sb("w_in", [P, D], F32)
        w_T = sb("w_T", [P, D], F32)
        bias_row = sb("bias_row", [P, D], F32)
        b_col = sb("b_col", [P, 1], F32)
        tanh_scale = sb("tanh_scale", [P, 1], F32)
        shift_col = sb("shift_col", [P, 1], F32)
        ident = sb("ident", [P, P], F32)
        ident_b = sb("ident_b", [P, P], BF16)
        neg_half = sb("neg_half", [P, SUB], F32)
        pos_half = sb("pos_half", [P, SUB], F32)
        eps_col = sb("eps_col", [P, SUB], F32)
        code_shift = sb("code_shift", [P, 2], F32)
        value_col = sb("value_col", [P, 1], F32)

        S = [ps(f"S{i}", [P, 2 * BLK], F32) for i in range(2)]
        O = ps("O", [P, 2, 512], F32)
        AT = ps("AT", [P, 2 * BLK], BF16)
        TQ = ps("TQ", [P, BLK], F32)
        hnT_ps = [S[1][:, 0:BLK], S[1][:, BLK:2 * BLK]]
        hT_ps = [S[0][:, 0:BLK], S[0][:, BLK:2 * BLK]]
        v_ps = [O[:, 0, :], O[:, 1, :]]

        names = """const_loaded zeros_ready idents_ready scale_ready wT_ready w_ready
            g_stats g_mv g_var g_rstd g_pre g_h g_ss g_inv g_unit g_T g_hi g_lo g_hT g_v g_vhi g_vlo
            y_loaded0 y_loaded1 y_ss y_ss_max y_inv y_unit_ready y_T y_hi y_lo y_vhi y_vlo
            adj_loaded0 adj_loaded1 packed_ready at_ready mask_ready scores_ready scores_free exp_ready
            wts_ready lo_ready pv_done o_half o_free
            xres_loaded xres_ready inv_sum_ready x1_ready stats_ready mv_ready var_ready rstd_ready
            centred hpre_ready h_ready ss_sum_ready ss_ready inv_ready hn_ready half_ready base_ready q_T q_hi q_ready
            inv_out_ready inv_half_ready res_ready stored""".split() + [f"x_loaded{g}" for g in range(NB)]
        s_ = {n: sem(n) for n in names}

        def wait(eng, name, value):
            if isinstance(value, int) and value <= 0:
                return
            eng.wait_ge(s_[name], value)

        adj_blocks = adj.rearrange("(s u p) j -> s p u j", u=SUB, p=P)
        x_blocks = x.rearrange("(s u p) d -> s p u d", u=SUB, p=P)
        y_blocks = y.rearrange("(s u p) d -> s p u d", u=SUB, p=P)
        out_blocks = out.rearrange("(s u p) d -> s p u d", u=SUB, p=P)

        def block_of(dram, s):
            return dram[bass.ds(s, 1)].rearrange("s p u d -> (s p) u d") if not isinstance(s, int) else dram[s]

        def phases(eng, run):
            run(0, 0, 0, None, None)
            run(0, 1, 1, 0, 0)
            run(1, 0, 2, 0, None)
            with eng.Fori(2, NB - 1) as s:
                run(0, s, 2 * s - 1, 1, s - 1)
                run(1, s - 1, 2 * s, 0, None)
            run(0, NB - 1, 2 * NB - 3, 1, NB - 2)
            run(1, NB - 2, 2 * NB - 2, 0, NB - 1)
            run(1, NB - 1, 2 * NB - 1, 1, None)

        def pairs(eng, step, p, before, hidden):
            special = isinstance(p, int) and p < 2 or hidden is not None and before == 0
            head = ITERS - 1 if special else 2 if before == 1 else 1
            for it in range(head):
                for kk in range(UNROLL):
                    step(it, kk, it == 0, False)
            if head < ITERS - 1:
                with eng.Fori(head, ITERS - 1) as it:
                    for kk in range(UNROLL):
                        step(it, kk, False, False)
            for kk in range(UNROLL):
                step(ITERS - 1, kk, False, True)

        def place(it, kk, before):
            return UNROLL * it + kk - (0 if before == 1 else LAG) if isinstance(it, int) else None

        def mask_pair(s, k):
            first = (s % 2) * NT + 2 * k
            return mask[:, :, :, :].rearrange("p a t i -> p (a t) i")[:, bass.ds(first, 2), :]

        def own_mask(s):
            return isinstance(s, int) and s < 2

        def masks_ahead(s):
            return not (isinstance(s, int) and s >= NB - 2)

        def y_group_at(p, it, kk, ahead=0):
            if not isinstance(p, int) or p > 1:
                return None
            pair = PAIRS * p + UNROLL * it + kk + ahead
            return y_pairs.index(pair) if pair in y_pairs else None

        def queries_at(before):
            return 0 if before == 1 else 1

        def block_before(layer, s, before):
            return {(0, 0): s - 1, (1, 0): s + 1, (0, 1): s - 2, (1, 1): s - 1}[(layer, before)]

        y_pairs = [3 + g * (2 * PAIRS - UNROLL - 3) // NB for g in range(NB)]

        block = ctx.enter_context(nc.Block())

        @block.sync
        def _(sp):
            for g in range(2):
                sp.dma_start(hg[g], x_blocks[g]).then_inc(s_[f"x_loaded{g}"], 16)
            sp.dma_start(w_in[:, :], W).then_inc(s_["const_loaded"], 16)
            sp.dma_start(bias_row[:, :], bias.rearrange("(a d) -> a d", a=1).to_broadcast((P, D))).then_inc(
                s_["const_loaded"], 16)
            sp.dma_start(b_col[:, :], b.rearrange("(a d) -> a d", a=1).to_broadcast((P, 1))).then_inc(
                s_["const_loaded"], 16)
            for g in range(2, NB):
                sp.dma_start(hg[g], x_blocks[g]).then_inc(s_[f"x_loaded{g}"], 16)
            sp.dma_start(x_res[:, :, :], x_blocks[0]).then_inc(s_["xres_loaded"], 16)

            def load_y(g):
                wait(sp, "y_vhi", g - 1)
                sp.dma_start(y_in[g % 2], y_blocks[g]).then_inc(s_[f"y_loaded{g % 2}"], 16)

            def load_adj(s, c):
                wait(sp, "at_ready", 2 * (CHUNKS * s + c) - 2)
                sp.dma_start(adj_in[c % 2][:, :, :],
                             block_of(adj_blocks, s)[:, :, c * CHUNK:(c + 1) * CHUNK]).then_inc(
                    s_[f"adj_loaded{c % 2}"], 16)

            def load_packed(s, c):
                if isinstance(s, int) and s == 2 and c < 2:
                    sp.wait_ge(s_["at_ready"], 2 * PAIRS - 2 + 2 * c)
                else:
                    sp.wait_ge(s_["packed_ready"], CHUNKS * (s - 2) + c - 1)
                sp.dma_start(adj_in[c % 2][:, :, :],
                             block_of(adj_blocks, s)[:, :, c * CHUNK:(c + 1) * CHUNK]).then_inc(
                    s_[f"adj_loaded{c % 2}"], 16)

            load_adj(0, 0)
            load_adj(0, 1)
            load_y(0)
            load_y(1)
            for n in range(2, 2 * CHUNKS):
                load_adj(n // CHUNKS, n % CHUNKS)
                for g in range(2, NB):
                    if y_pairs[g - 2] // 2 + 1 == n - 1:
                        load_y(g)
            for c in range(CHUNKS):
                load_packed(2, c)
            with sp.Fori(3, NB) as s:
                for c in range(CHUNKS):
                    load_packed(s, c)

        @block.tensor
        def _(pe):
            pe.wait_ge(s_["idents_ready"], 1)
            pe.wait_ge(s_["const_loaded"], 48)
            nc.tensor.transpose(TQ[:, 0:P], w_in[:, :], ident[:, :]).then_inc(s_["wT_ready"], 1)

            def start_turn(g):
                pe.wait_ge(s_["g_unit"], 1 + g)
                wait(pe, "g_hi", g - 1)
                wait(pe, "g_lo", g - 1)
                for u in range(SUB):
                    nc.tensor.transpose(hnT_ps[g % 2][:, u * P:(u + 1) * P], hng[g % RING][:, u, :], ident[:, :])
                for u in range(SUB):
                    last = nc.tensor.transpose(hT_ps[g % 2][:, u * P:(u + 1) * P], hg[g][:, u, :], ident[:, :])
                last.then_inc(s_["g_T"], 1)

            def start_values(g):
                pe.wait_ge(s_["g_hT"], 1 + g)
                if g == 0:
                    pe.wait_ge(s_["w_ready"], 1)
                wait(pe, "g_vlo", g - 1)
                for u in range(SUB):
                    last = nc.tensor.matmul(v_ps[g % 2][:, u * P:(u + 1) * P], hT[g % RING][:, u * P:(u + 1) * P],
                                            w_T[:, :], start=True, stop=True)
                last.then_inc(s_["g_v"], 1)

            for t in range(NB + 1):
                if t < NB:
                    start_turn(t)
                if t >= 1:
                    start_values(t - 1)

            def turn_y(g):
                pe.wait_ge(s_["y_unit_ready"], g + 1)
                wait(pe, "y_lo", g)
                for u in range(SUB):
                    last = nc.tensor.transpose(TQ[:, u * P:(u + 1) * P], y_unit[:, u, :], ident[:, :])
                last.then_inc(s_["y_T"], 1)

            def scores(layer, s, G, k, kk):
                wait(pe, "scores_free", G - 1)
                dst = S[kk % 2]
                for jj in range(2):
                    cols = bass.ds((2 * k + jj) * P, P)
                    k_hi, k_lo = keys_hi[layer][:, cols], keys_lo[layer][:, cols]
                    if layer == 0:
                        q_hi = keys_hi[0][:, bass.ds(s * BLK, BLK)]
                        q_lo = keys_lo[0][:, bass.ds(s * BLK, BLK)]
                    else:
                        q = q_last if isinstance(s, int) and s == NB - 1 else q_sb
                        q_hi, q_lo = q[:, 0, :], q[:, 1, :]
                    o = dst[:, jj * BLK:(jj + 1) * BLK]
                    nc.tensor.matmul(o, k_hi, q_hi, start=True, stop=False)
                    nc.tensor.matmul(o, k_hi, q_lo, start=False, stop=False)
                    last = nc.tensor.matmul(o, k_lo, q_hi, start=False, stop=True)
                last.then_inc(s_["scores_ready"], 1)

            def turn_packed(s, it, kk):
                c = 2 * it + kk // 2
                pe.wait_ge(s_["packed_ready"], CHUNKS * (s - 2) + c + 1)
                pe.wait_ge(s_["mask_ready"], PAIRS * s + 2 * c - 1)
                for jj in range(2):
                    for u in range(SUB):
                        last = nc.tensor.transpose(AT[:, (jj * SUB + u) * P:(jj * SUB + u + 1) * P],
                                                   packed[kk // 2][:, u, jj * P:(jj + 1) * P], ident_b[:, :])
                last.then_inc(s_["at_ready"], 1)

            def turn_adj(s, it, kk):
                if kk % 2 == 0:
                    pe.wait_ge(s_[f"adj_loaded{kk // 2}"], 16 * (ITERS * s + it + 1))
                wait(pe, "mask_ready", PAIRS * s + UNROLL * it + kk)
                src = adj_in[kk // 2][:, :, :].bitcast(BF16).rearrange("p u (j two) -> p u two j", two=2)
                for jj in range(2):
                    for u in range(SUB):
                        c0 = (2 * (kk % 2) + jj) * P
                        last = nc.tensor.transpose(AT[:, (jj * SUB + u) * P:(jj * SUB + u + 1) * P],
                                                   src[:, u, 1, c0:c0 + P], ident_b[:, :])
                last.then_inc(s_["at_ready"], 1)

            def products(layer, p, G, k, slot):
                first = isinstance(k, int) and k == 0
                final = isinstance(k, int) and k == PAIRS - 1
                pe.wait_ge(s_["lo_ready"], G + 1)
                hi = wts[slot][:, :].bitcast(BF16).rearrange("p (c two) -> p two c", two=2)
                for u in range(SUB):
                    o = O[:, u // 2, (u % 2) * (D + 1):(u % 2 + 1) * (D + 1)]
                    if first and u % 2 == 0:
                        wait(pe, "o_free", 0 if isinstance(p, int) and p == 0 else 2 * p - 1 + u // 2)
                    for jj in range(2):
                        c0 = jj * BLK + u * P
                        tile = 2 * k + jj
                        if isinstance(k, int):
                            v = vals[layer][:, tile, :]
                        else:
                            v = vals[layer][:, bass.ds(tile, 1), :].rearrange("p a c -> p (a c)")
                        w_hi, w_lo = hi[:, 1, c0:c0 + P], wts_lo[slot][:, c0:c0 + P]
                        nc.tensor.matmul(o, w_hi, v[:, 0:D + 1], start=first and jj == 0 and u % 2 == 0,
                                         stop=False, skip_group_check=True)
                        nc.tensor.matmul(o[:, 0:D], w_hi, v[:, D + 2:VCOL], start=False, stop=False,
                                         skip_group_check=True)
                        last = nc.tensor.matmul(o, w_lo, v[:, 0:D + 1], start=False, stop=final and jj == 1,
                                                skip_group_check=True)
                    if final and u == 1:
                        last.then_inc(s_["o_half"], 1)
                last.then_inc(s_["pv_done"], 1)

            def turn_queries(n):
                pe.wait_ge(s_["hn_ready"], n + 1)
                pe.wait_ge(s_["y_lo"], NB)
                wait(pe, "q_ready", n)
                for u in range(SUB):
                    last = nc.tensor.transpose(TQ[:, u * P:(u + 1) * P], hn1[:, u, :], ident[:, :])
                last.then_inc(s_["q_T"], 1)

            def run(layer, s, p, before, hidden):
                if layer == 1:
                    pe.wait_ge(s_["q_ready"], s + 1)
                if isinstance(p, int) and p == 2:
                    pe.wait_ge(s_["y_vlo"], NB)

                def step(it, kk, first, last):
                    k = UNROLL * it + kk
                    G = PAIRS * p + k
                    g = y_group_at(p, it, kk)
                    if g is not None:
                        turn_y(g)
                    if hidden is not None and last and kk == queries_at(before):
                        turn_queries(hidden)
                    if layer == 0 and own_mask(s):
                        turn_adj(s, it, kk)
                    if before is None and first and kk == 1:
                        pe.wait_ge(s_["g_lo"], NB)
                    if before is None and first and kk == LAG:
                        pe.wait_ge(s_["g_vlo"], NB)
                    scores(layer, s, G, k, kk)
                    if not first or kk >= LAG:
                        products(layer, p, G - LAG, k - LAG, (kk - LAG) % UNROLL)
                    elif before is not None:
                        products(before, p - 1, G - LAG, PAIRS - LAG + kk, UNROLL - LAG + kk)
                    if layer == 1 and masks_ahead(s) and kk % 2 == 1:
                        turn_packed(s + 2, it, kk)

                pairs(pe, step, p, before, hidden)

            phases(pe, run)
            for kk in range(LAG):
                products(1, 2 * NB - 1, 2 * NB * PAIRS - LAG + kk, PAIRS - LAG + kk, UNROLL - LAG + kk)

        @block.scalar
        def _(act):
            act.wait_ge(s_["wT_ready"], 1)
            nc.scalar.activation(w_T[:, :], TQ[:, 0:P], ACT.Copy, scale=VALUE).then_inc(s_["w_ready"], 1)

            def start_h(g):
                act.wait_ge(s_["g_pre"], g + 1)
                nc.scalar.activation(hg[g], hg[g], ACT.Relu).then_inc(s_["g_h"], 1)
                act.wait_ge(s_["g_h"], g + 1)
                wait(act, "g_T", g - RING + 1)
                for u in range(SUB):
                    last = nc.scalar.activation(hng[g % RING][:, u, :], hg[g][:, u, :], ACT.Square,
                                                scale=1.0 / UNIT, accum_out=ss_g[:, g, u:u + 1])
                last.then_inc(s_["g_ss"], 1)

            def start_keys(g):
                act.wait_ge(s_["g_T"], g + 1)
                wait(act, "g_v", g - RING + 1)
                nc.scalar.activation(hT[g % RING], hT_ps[g % 2], ACT.Copy).then_inc(s_["g_hT"], 1)
                nc.scalar.activation(keys_hi[0][:, g * BLK:(g + 1) * BLK], hnT_ps[g % 2], ACT.Copy).then_inc(
                    s_["g_hi"], 1)

            def start_values(g):
                act.wait_ge(s_["g_v"], g + 1)
                nc.scalar.activation(vals[0][:, g * SUB:(g + 1) * SUB, 0:D],
                                     v_ps[g % 2].rearrange("p (u d) -> p u d", u=SUB), ACT.Copy).then_inc(
                    s_["g_vhi"], 1)

            for t in range(NB + 3):
                if t < NB:
                    start_h(t)
                if 2 <= t < NB + 2:
                    start_keys(t - 2)
                if t >= 3:
                    start_values(t - 3)

            def mask_out(s, k, kk):
                act.wait_ge(s_["at_ready"], PAIRS * s + k + 1)
                if kk % 2 == 0:
                    nc.scalar.activation(mask_pair(s, k), AT[:, :].rearrange("p (t i) -> p t i", t=2), ACT.Square,
                                         bias=code_shift[:, 0:1]).then_inc(s_["mask_ready"], 1)
                else:
                    nc.scalar.activation(mask_pair(s, k), AT[:, :].rearrange("p (t i) -> p t i", t=2),
                                         ACT.Copy).then_inc(s_["mask_ready"], 1)

            def mask_unpacked(s, k, c, kk):
                if kk % 2 == 0:
                    act.wait_ge(s_["at_ready"], 2 * PAIRS + CHUNKS * (s - 2) + c + 1)
                    nc.scalar.activation(mask_pair(s, k), AT[:, :].rearrange("p (t i) -> p t i", t=2), ACT.Square,
                                         bias=code_shift[:, 0:1]).then_inc(s_["mask_ready"], 1)
                else:
                    act.wait_ge(s_["mask_ready"], PAIRS * s + k)
                    nc.scalar.activation(mask_pair(s, k), mask_pair(s, k - 1), ACT.Square,
                                         bias=code_shift[:, 1:2]).then_inc(s_["mask_ready"], 1)

            def store(n):
                act.wait_ge(s_["res_ready"], n + 1)
                act.dma_start(block_of(out_blocks, n), res[:, :, :]).then_inc(s_["stored"], 16)

            def evacuate(layer, n, p):
                wait(act, "x1_ready" if layer == 0 else "res_ready", n)
                for half in range(2):
                    if half == 0:
                        act.wait_ge(s_["o_half"], p + 1)
                    else:
                        act.wait_ge(s_["pv_done"], PAIRS * (p + 1))
                    nc.scalar.activation(raw[layer][:, 2 * half:2 * half + 2, :],
                                         O[:, half, 0:2 * (D + 1)].rearrange("p (u c) -> p u c", u=2),
                                         ACT.Copy).then_inc(s_["o_free"], 1)

            def hidden_h(n):
                act.wait_ge(s_["hpre_ready"], n + 1)
                nc.scalar.activation(h1[:, :, :], h1[:, :, :], ACT.Relu).then_inc(s_["h_ready"], 1)

            def hidden_squares(n, part):
                act.wait_ge(s_["h_ready"], n + 1)
                for u in (2 * part, 2 * part + 1):
                    last = nc.scalar.activation(hn1[:, u, :], h1[:, u, :], ACT.Square, scale=1.0 / UNIT,
                                                accum_out=ss[:, u:u + 1])
                last.then_inc(s_["ss_sum_ready"], 1)

            def run(layer, s, p, before, hidden):
                def step(it, kk, first, last):
                    k = UNROLL * it + kk
                    G = PAIRS * p + k
                    if layer == 0 and own_mask(s):
                        mask_out(s, k, kk)
                    elif layer == 1 and masks_ahead(s) and not (first and kk < 2):
                        act.wait_ge(s_["wts_ready"], G - 1)
                        mask_unpacked(s + 2, k - 2, 2 * it + kk // 2 - 1, kk)
                    elif layer == 0 and last and kk < 2:
                        mask_unpacked(s, PAIRS - 2 + kk, CHUNKS - 1, kk)
                    act.wait_ge(s_["scores_ready"], G + 1)
                    wait(act, "pv_done", G - UNROLL + 1)
                    e = wts[kk][:, :]
                    if layer == 0:
                        nc.scalar.activation(e, S[kk % 2][:, :], ACT.Tanh, scale=tanh_scale[:, 0:1]).then_inc(
                            s_["scores_free"], 1)
                        act.wait_ge(s_["scores_free"], G + 1)
                        nc.scalar.activation(e, e, ACT.Exp, scale=8.0, bias=shift_col[:, 0:1]).then_inc(
                            s_["exp_ready"], 1)
                    else:
                        nc.scalar.activation(e, S[kk % 2][:, :], ACT.Exp, scale=COS).then_inc(
                            s_["scores_free"], 1)
                    if first and kk == LAG - 1 and before is not None:
                        evacuate(before, block_before(layer, s, before), p - 1)
                    g = y_group_at(p, it, kk)
                    if g is not None:
                        act.wait_ge(s_["y_T"], g + 1)
                        nc.scalar.activation(keys_hi[1][:, bass.ds(g * BLK, BLK)], TQ[:, :], ACT.Copy).then_inc(
                            s_["y_hi"], 1)
                    if hidden is not None and place(it, kk, before) == 5:
                        hidden_h(hidden)
                    if hidden is not None and place(it, kk, before) in (6, 7):
                        hidden_squares(hidden, place(it, kk, before) - 6)
                    if hidden is not None and last and kk == queries_at(before):
                        act.wait_ge(s_["q_T"], hidden + 1)
                        q = q_last if isinstance(hidden, int) and hidden == NB - 1 else q_sb
                        nc.scalar.activation(q[:, 0, :], TQ[:, :], ACT.Copy).then_inc(s_["q_hi"], 1)

                pairs(act, step, p, before, hidden)
                if layer == 0 and not (isinstance(s, int) and s == 0):
                    act.wait_ge(s_["x1_ready"], s)
                    act.dma_start(x_res[:, :, :], block_of(x_blocks, s)).then_inc(s_["xres_loaded"], 16)
                if before == 1:
                    store(block_before(layer, s, before))

            act.wait_ge(s_["scale_ready"], 1)
            phases(act, run)
            evacuate(1, NB - 1, 2 * NB - 1)
            store(NB - 1)
            act.wait_ge(s_["stored"], 16 * NB)

        @block.vector
        def _(dve):
            def start_stats(g):
                dve.wait_ge(s_[f"x_loaded{g}"], 16)
                for u in range(SUB):
                    last = nc.vector.bn_stats(stats_g[g][:, u, :], hg[g][:, u, :])
                last.then_inc(s_["g_stats"], 1)

            def start_mv(g):
                dve.wait_ge(s_["g_stats"], g + 1)
                for u in range(SUB):
                    last = nc.vector.bn_aggr(mv_g[g][:, u, :], stats_g[g][:, u, :])
                last.then_inc(s_["g_mv"], 1)
                dve.wait_ge(s_["g_mv"], g + 1)
                nc.vector.tensor_scalar(rstd_g[:, g, :], mv_g[g][:, :, 1], LN_EPS, None, ALU.add).then_inc(
                    s_["g_var"], 1)

            def start_norm(g):
                dve.wait_ge(s_["g_rstd"], g + 1)
                for u in range(SUB):
                    last = nc.vector.tensor_scalar(hg[g][:, u, :], hg[g][:, u, :], mv_g[g][:, u, 0:1],
                                                   rstd_g[:, g, u:u + 1], ALU.subtract, ALU.mult)
                last.then_inc(s_["g_pre"], 1)

            def start_keys(g):
                dve.wait_ge(s_["g_hi"], g + 1)
                cols = slice(g * BLK, (g + 1) * BLK)
                nc.vector.tensor_tensor(keys_lo[0][:, cols], hnT_ps[g % 2], keys_hi[0][:, cols],
                                        ALU.subtract).then_inc(s_["g_lo"], 1)

            def start_values(g):
                dve.wait_ge(s_["g_vhi"], g + 1)
                tiles = slice(g * SUB, (g + 1) * SUB)
                nc.vector.tensor_tensor(vals[0][:, tiles, D + 2:VCOL],
                                        v_ps[g % 2].rearrange("p (u d) -> p u d", u=SUB),
                                        vals[0][:, tiles, 0:D], ALU.subtract).then_inc(s_["g_vlo"], 1)

            start_stats(0)
            for t in range(NB + 5):
                if t + 1 < NB:
                    start_stats(t + 1)
                if t < NB:
                    start_mv(t)
                if 1 <= t <= NB:
                    start_norm(t - 1)
                if 4 <= t < NB + 4:
                    start_keys(t - 4)
                if t >= 5:
                    start_values(t - 5)

            def y_squares(g):
                dve.wait_ge(s_[f"y_loaded{g % 2}"], 16 * (g // 2 + 1))
                wait(dve, "y_inv", g)
                for u in range(SUB):
                    last = nc.vector.tensor_tensor_reduce(out=half_h[:, u, :], in0=y_in[g % 2][:, u, :],
                                                          in1=y_in[g % 2][:, u, :], scale=COS, scalar=0.0,
                                                          op0=ALU.mult, op1=ALU.add, accum_out=ssy[:, u:u + 1])
                last.then_inc(s_["y_ss"], 1)
                dve.wait_ge(s_["y_ss"], g + 1)
                nc.vector.tensor_scalar(ssy[:, :], ssy[:, :], NORM_EPS ** 2 * COS, None, ALU.max).then_inc(
                    s_["y_ss_max"], 1)

            def y_low(g):
                dve.wait_ge(s_["y_hi"], g + 1)
                cols = bass.ds(g * BLK, BLK)
                nc.vector.tensor_tensor(keys_lo[1][:, cols], TQ[:, :], keys_hi[1][:, cols],
                                        ALU.subtract).then_inc(s_["y_lo"], 1)

            def hidden_part(at, n, p):
                if at == 0:
                    dve.wait_ge(s_["o_free"], 2 * (p + 1))
                    nc.vector.reciprocal(inv_sum[0][:, :], raw[0][:, :, D]).then_inc(s_["inv_sum_ready"], 1)
                elif at == 1:
                    dve.wait_ge(s_["inv_sum_ready"], n + 1)
                    dve.wait_ge(s_["xres_ready"], n + 1)
                    wait(dve, "base_ready", n)
                    for u in range(SUB):
                        last = nc.vector.scalar_tensor_tensor(out=x1[:, u, :], in0=raw[0][:, u, 0:D],
                                                              scalar=inv_sum[0][:, u:u + 1], in1=x_res[:, u, :],
                                                              op0=ALU.mult, op1=ALU.add)
                    last.then_inc(s_["x1_ready"], 1)
                elif at == 2:
                    dve.wait_ge(s_["x1_ready"], n + 1)
                    for u in range(SUB):
                        last = nc.vector.bn_stats(stats[:, u, :], x1[:, u, :])
                    last.then_inc(s_["stats_ready"], 1)
                elif at == 3:
                    for u in range(SUB):
                        last = nc.vector.bn_aggr(mv[:, u, :], stats[:, u, :])
                    last.then_inc(s_["mv_ready"], 1)

            def finish_scale(n, p):
                dve.wait_ge(s_["o_free"], 2 * (p + 1))
                nc.vector.reciprocal(inv_sum[1][:, :], raw[1][:, :, D]).then_inc(s_["inv_out_ready"], 1)
                dve.wait_ge(s_["inv_out_ready"], n + 1)
                nc.vector.tensor_scalar(inv_sum[1][:, :], inv_sum[1][:, :], 0.5, None, ALU.mult).then_inc(
                    s_["inv_half_ready"], 1)

            def finish(n):
                dve.wait_ge(s_["inv_half_ready"], n + 1)
                dve.wait_ge(s_["base_ready"], n + 1)
                wait(dve, "stored", 16 * n)
                for u in range(SUB):
                    last = nc.vector.scalar_tensor_tensor(out=res[:, u, :], in0=raw[1][:, u, 0:D],
                                                          scalar=inv_sum[1][:, u:u + 1], in1=base[:, u, :],
                                                          op0=ALU.mult, op1=ALU.add)
                last.then_inc(s_["res_ready"], 1)

            def low_part(G, slot):
                dve.wait_ge(s_["wts_ready"], G + 1)
                w = wts[slot][:, :]
                hi = w.bitcast(BF16).rearrange("p (c two) -> p two c", two=2)[:, 1, :]
                nc.vector.tensor_tensor(wts_lo[slot][:, :], w, hi, ALU.subtract).then_inc(s_["lo_ready"], 1)

            def run(layer, s, p, before, hidden):
                p_sums = p - 1 if before == 0 else p - 2

                def step(it, kk, first, last):
                    k = UNROLL * it + kk
                    G = PAIRS * p + k
                    if layer == 0:
                        dve.wait_ge(s_["exp_ready"], PAIRS * s + k + 1)
                        dve.wait_ge(s_["mask_ready"], PAIRS * s + k + 1)
                    else:
                        dve.wait_ge(s_["scores_free"], G + 1)
                    w = wts[kk][:, :].rearrange("p (t i) -> p t i", t=2)
                    nc.vector.scalar_tensor_tensor(out=w, in0=mask_pair(s, k),
                                                   scalar=(1.0, 0.5)[kk % 2], in1=w,
                                                   op0=(ALU.is_lt, ALU.is_gt)[kk % 2],
                                                   op1=ALU.mult).then_inc(s_["wts_ready"], 1)
                    at = place(it, kk, before)
                    if hidden is not None and at == 3:
                        dve.wait_ge(s_["stats_ready"], hidden + 1)
                    low_part(G, kk)
                    if hidden is not None:
                        hidden_part(at, hidden, p_sums)
                    if before == 1 and at == LAG:
                        finish_scale(block_before(layer, s, before), p - 1)
                    if before == 1 and at == LAG + 1:
                        finish(block_before(layer, s, before))
                    g = y_group_at(p, it, kk)
                    if g is not None:
                        y_low(g)
                    g = y_group_at(p, it, kk, YAHEAD)
                    if g is not None and g > 0:
                        y_squares(g)
                    if hidden is not None and last and kk == queries_at(before):
                        dve.wait_ge(s_["q_hi"], hidden + 1)
                        q = q_last if isinstance(hidden, int) and hidden == NB - 1 else q_sb
                        nc.vector.tensor_tensor(q[:, 1, :], TQ[:, :], q[:, 0, :],
                                                ALU.subtract).then_inc(s_["q_ready"], 1)

                pairs(dve, step, p, before, hidden)

            y_squares(0)
            phases(dve, run)
            finish_scale(NB - 1, 2 * NB - 1)
            finish(NB - 1)

        @block.gpsimd
        def _(pool):
            nc.gpsimd.memset(ident[:, :], 0.0)
            nc.gpsimd.memset(ident_b[:, :], 0.0)
            nc.gpsimd.memset(neg_half[:, :], -0.5)
            nc.gpsimd.memset(pos_half[:, :], 0.5)
            nc.gpsimd.memset(eps_col[:, :], LN_EPS)
            nc.gpsimd.memset(value_col[:, :], VALUE)
            for at, shift in enumerate((-1.25, -1.0)):
                nc.gpsimd.memset(code_shift[:, at:at + 1], shift)
            nc.gpsimd.memset(shift_col[:, :], LOG_SHIFT)
            for l in range(2):
                last = nc.gpsimd.memset(vals[l][:, :, D:D + 1], VALUE)
            last.then_inc(s_["zeros_ready"], 1)
            pool.wait_ge(s_["zeros_ready"], 1)
            for m in (ident, ident_b):
                last = nc.gpsimd.affine_select(out=m[:, :], in_=m[:, :], compare_op=ALU.not_equal, fill=1.0,
                                               base=0, pattern=[[-1, P]], channel_multiplier=1)
            last.then_inc(s_["idents_ready"], 1)
            pool.wait_ge(s_["const_loaded"], 48)
            nc.gpsimd.tensor_scalar(tanh_scale[:, :], b_col[:, :], COS / 8.0, 1.0, ALU.mult, ALU.mult).then_inc(
                s_["scale_ready"], 1)

            def start_rstd(g):
                pool.wait_ge(s_["g_var"], g + 1)
                nc.gpsimd.tensor_tensor(rstd_g[:, g, :], rstd_g[:, g, :], neg_half[:, :], ALU.pow).then_inc(
                    s_["g_rstd"], 1)

            def start_unit(g):
                pool.wait_ge(s_["g_ss"], g + 1)
                nc.gpsimd.tensor_tensor(inv_g[:, g, :], ss_g[:, g, :], neg_half[:, :], ALU.pow).then_inc(
                    s_["g_inv"], 1)
                pool.wait_ge(s_["g_inv"], g + 1)
                nc.gpsimd.tensor_tensor(hng[g % RING], hg[g], inv_g[:, g, :].to_broadcast((P, SUB, D)),
                                        ALU.mult).then_inc(s_["g_unit"], 1)

            for t in range(NB + 2):
                if t < NB:
                    start_rstd(t)
                if t >= 2:
                    start_unit(t - 2)

            def residual(n):
                pool.wait_ge(s_["xres_loaded"], 16 * (n + 1))
                for u in range(SUB):
                    last = nc.gpsimd.tensor_tensor(x_res[:, u, :], x_res[:, u, :], bias_row[:, :], ALU.add)
                last.then_inc(s_["xres_ready"], 1)

            def y_group(g):
                pool.wait_ge(s_["y_ss_max"], g + 1)
                wait(pool, "y_unit_ready", g)
                nc.gpsimd.tensor_tensor(invy[:, :], ssy[:, :], neg_half[:, :], ALU.pow).then_inc(s_["y_inv"], 1)
                pool.wait_ge(s_["y_inv"], g + 1)
                wait(pool, "y_T", g)
                nc.gpsimd.tensor_tensor(y_unit[:, :, :], y_in[g % 2], invy[:, :].to_broadcast((P, SUB, D)),
                                        ALU.mult).then_inc(s_["y_unit_ready"], 1)
                wait(pool, "y_vlo", g)
                for values in (y_big[:, :, :], vals[1][:, bass.ds(g * SUB, SUB), 0:D]):
                    last = nc.gpsimd.tensor_tensor(values, y_in[g % 2],
                                                   value_col[:, :].to_broadcast((P, SUB, D)), ALU.mult)
                last.then_inc(s_["y_vhi"], 1)
                pool.wait_ge(s_["y_vhi"], g + 1)
                tiles = slice(g * SUB, (g + 1) * SUB)
                nc.gpsimd.tensor_tensor(vals[1][:, tiles, D + 2:VCOL], y_big[:, :, :], vals[1][:, tiles, 0:D],
                                        ALU.subtract).then_inc(s_["y_vlo"], 1)

            for g in range(NB):
                if g == ITERS:
                    residual(0)
                y_group(g)

            def pack(s):
                for c in range(CHUNKS):
                    pool.wait_ge(s_[f"adj_loaded{c % 2}"], 16 * (CHUNKS // 2 * s + c // 2 + 1))
                    wait(pool, "at_ready", 2 * PAIRS + CHUNKS * (s - 2) + c - 1)
                    a = adj_in[c % 2][:, :, 0:CHUNK // 2].bitcast(F16).rearrange("p u (j two) -> p u two j", two=2)
                    nc.gpsimd.tensor_tensor(packed[c % 2], a[:, :, 1, :], adj_in[c % 2][:, :, CHUNK // 2:CHUNK],
                                            ALU.subtract).then_inc(s_["packed_ready"], 1)

            def hidden_norm(n):
                pool.wait_ge(s_["mv_ready"], n + 1)
                nc.gpsimd.tensor_tensor(rstd[:, :], mv[:, :, 1], eps_col[:, :], ALU.add).then_inc(
                    s_["var_ready"], 1)
                nc.gpsimd.tensor_tensor(h1[:, :, :], x1[:, :, :], mv[:, :, 0:1].to_broadcast((P, SUB, D)),
                                        ALU.subtract).then_inc(s_["centred"], 1)
                pool.wait_ge(s_["var_ready"], n + 1)
                nc.gpsimd.tensor_tensor(rstd[:, :], rstd[:, :], neg_half[:, :], ALU.pow).then_inc(
                    s_["rstd_ready"], 1)
                pool.wait_ge(s_["centred"], n + 1)
                pool.wait_ge(s_["rstd_ready"], n + 1)
                nc.gpsimd.tensor_tensor(h1[:, :, :], h1[:, :, :], rstd[:, :].to_broadcast((P, SUB, D)),
                                        ALU.mult).then_inc(s_["hpre_ready"], 1)

            def hidden_unit(n):
                pool.wait_ge(s_["ss_sum_ready"], 2 * n + 2)
                nc.gpsimd.tensor_tensor(half_h[:, :, :], h1[:, :, :], pos_half[:, 0:1].to_broadcast((P, SUB, D)),
                                        ALU.mult).then_inc(s_["half_ready"], 1)
                nc.gpsimd.tensor_scalar(ss[:, :], ss[:, :], NORM_EPS ** 2 * COS, 3e38, ALU.max,
                                        ALU.min).then_inc(s_["ss_ready"], 1)
                pool.wait_ge(s_["ss_ready"], n + 1)
                nc.gpsimd.tensor_tensor(inv[:, :], ss[:, :], neg_half[:, :], ALU.pow).then_inc(s_["inv_ready"], 1)
                wait(pool, "q_T", n)
                pool.wait_ge(s_["inv_ready"], n + 1)
                nc.gpsimd.tensor_tensor(hn1[:, :, :], h1[:, :, :], inv[:, :].to_broadcast((P, SUB, D)),
                                        ALU.mult).then_inc(s_["hn_ready"], 1)

            def residual_out(n):
                wait(pool, "res_ready", n)
                pool.wait_ge(s_["half_ready"], n + 1)
                nc.gpsimd.tensor_tensor(base[:, :, :], half_h[:, :, :], x1[:, :, :], ALU.add).then_inc(
                    s_["base_ready"], 1)

            hidden_norm(0)
            hidden_unit(0)
            residual_out(0)
            pool.wait_ge(s_["y_T"], NB)
            pack(2)
            with pool.Fori(1, NB - 2) as n:
                residual(n)
                hidden_norm(n)
                hidden_unit(n)
                residual_out(n)
                pack(n + 2)
            with pool.Fori(NB - 2, NB) as n:
                residual(n)
                hidden_norm(n)
                hidden_unit(n)
                residual_out(n)


_INS = ['x', 'adj', 'L0_gnn_W', 'L0_gnn_bias', 'L0_gnn_b', 'L1_gnn_y']
_OUTS = [((4096, 128), 'float32')]


def kernel(**inputs):
    import numpy as _np
    import concourse.bacc as _bacc
    from concourse import mybir as _mybir
    from concourse.bass_utils import run_bass_kernel_spmd as _run

    nc = _bacc.Bacc("TRN2", target_bir_lowering=False, num_devices=1)
    arrays, args = {}, []
    for name in _INS:
        a = _np.ascontiguousarray(inputs[name])
        arrays[f"in_{name}_dram"] = a
        args.append(nc.dram_tensor(f"in_{name}_dram", a.shape, _mybir.dt.from_np(a.dtype), kind="ExternalInput").ap())
    for i, (shape, dtype) in enumerate(_OUTS):
        dt = _mybir.dt.from_np(_np.dtype(dtype))
        args.append(nc.dram_tensor(f"out_{i}_dram", shape, dt, kind="ExternalOutput").ap())
    two_layers(nc, *args)
    r = _run(nc, [arrays], core_ids=[0])
    return r.results[0]["out_0_dram"]
```
